# Optimizing a Trainium2 kernel written in Bass

```python
import numpy as np
import jax
import jax.numpy as jnp

def _softmax(x, axis=-1):
    return jax.nn.softmax(x, axis=axis)

def _gelu(x):
    return jax.nn.gelu(x, approximate=True)

def _silu(x):
    return jax.nn.silu(x)

def _sigmoid(x):
    return jax.nn.sigmoid(x)

def _layernorm(x, axis=-1, eps=1e-05):
    m = jnp.mean(x, axis=axis, keepdims=True)
    v = jnp.var(x, axis=axis, keepdims=True)
    return (x - m) / jnp.sqrt(v + eps)

def _scatter_add(tgt, idx, src, axis=0):
    return tgt.at[idx].add(src)

def _segment_sum(src, seg, n):
    return jax.ops.segment_sum(src, seg, n)
kernel_name = 'mk_adj_preln_d2_adj_r2_e06740'

def setup_inputs(seed: int=0):
    np.random.seed(seed)
    _w = jnp.asarray

    def _rec_inputs():
        import jax
        import jax.numpy as jnp
        _gk = jax.random.key(seed)
        x = 7.22e-05 + 1 * jax.random.normal(jax.random.fold_in(_gk, 1), (16, 512, 256), jnp.float32)
        _a = jax.random.bernoulli(jax.random.fold_in(_gk, 2), 0.0078125, (16, 512, 512))
        _a = jnp.logical_or(_a, jnp.swapaxes(_a, -1, -2))
        _a = jnp.logical_or(_a, jnp.eye(512, dtype=bool))
        _af = _a.astype(jnp.float32)
        _af = _af * jax.random.uniform(jax.random.fold_in(_gk, 3), (16, 512, 512), jnp.float32, 0.05, 1)
        adj = _af
        _nm = jnp.ones((16, 512), dtype=bool)
        nodemask = jnp.where(_nm, 1.0, 0.0).astype(jnp.float32)
        return (x, adj, nodemask)
    x, adj, nodemask = _rec_inputs()

    def _L0_gnn_setup():
        import jax, jax.numpy as jnp
        import numpy as np
        B, N, D = (8, 1024, 256)
        key = jax.random.key(seed)
        ks = jax.random.split(key, 8)
        scale = 0.5 / np.sqrt(D)
        x = jax.random.normal(ks[0], (B, N, D), dtype=jnp.float32)
        adj = jax.random.uniform(ks[1], (B, N, N), dtype=jnp.float32)
        Wq_w = jax.random.normal(ks[2], (D, D), dtype=jnp.float32) * scale
        Wk_w = jax.random.normal(ks[3], (D, D), dtype=jnp.float32) * scale
        Wv_w = jax.random.normal(ks[4], (D, D), dtype=jnp.float32) * scale
        Wq_b = jnp.zeros((D,), dtype=jnp.float32)
        Wk_b = jnp.zeros((D,), dtype=jnp.float32)
        Wv_b = jnp.zeros((D,), dtype=jnp.float32)
        return {'x': x, 'adj': adj, 'Wq_w': Wq_w, 'Wq_b': Wq_b, 'Wk_w': Wk_w, 'Wk_b': Wk_b, 'Wv_w': Wv_w, 'Wv_b': Wv_b}
    _L0_gnn_all = _L0_gnn_setup()
    _L0_gnn_in = {k: v for k, v in _L0_gnn_all.items() if k in ('Wq_w', 'Wq_b', 'Wk_w', 'Wk_b', 'Wv_w', 'Wv_b')}
    del _L0_gnn_all

    def _L1_gnn_setup():
        import jax, jax.numpy as jnp
        import numpy as np
        B, N, IN_DIM, ATT_DIM = (2, 4096, 256, 256)
        key = jax.random.key(seed)
        k1, k2, k3, k4 = jax.random.split(key, 4)
        X = jax.random.normal(k1, (B, N, IN_DIM), dtype=jnp.float32)
        adj = jax.random.uniform(k2, (B, N, N), dtype=jnp.float32)
        mask = jnp.ones((B, N), dtype=jnp.float32)
        Wqk = jax.random.normal(k3, (IN_DIM, 2 * ATT_DIM), dtype=jnp.float32) / np.sqrt(IN_DIM)
        Wv = jax.random.normal(k4, (IN_DIM, IN_DIM), dtype=jnp.float32) / np.sqrt(IN_DIM)
        return {'X': X, 'adj': adj, 'mask': mask, 'Wqk': Wqk, 'Wv': Wv}
    _L1_gnn_all = _L1_gnn_setup()
    _L1_gnn_in = {k: v for k, v in _L1_gnn_all.items() if k in ('Wqk', 'Wv')}
    del _L1_gnn_all
    return {'x': x, 'adj': adj, 'nodemask': nodemask, 'L0_gnn_Wq_w': _L0_gnn_in['Wq_w'], 'L0_gnn_Wq_b': _L0_gnn_in['Wq_b'], 'L0_gnn_Wk_w': _L0_gnn_in['Wk_w'], 'L0_gnn_Wk_b': _L0_gnn_in['Wk_b'], 'L0_gnn_Wv_w': _L0_gnn_in['Wv_w'], 'L0_gnn_Wv_b': _L0_gnn_in['Wv_b'], 'L1_gnn_Wqk': _L1_gnn_in['Wqk'], 'L1_gnn_Wv': _L1_gnn_in['Wv']}

def reference(x, adj, nodemask, L0_gnn_Wq_w, L0_gnn_Wq_b, L0_gnn_Wk_w, L0_gnn_Wk_b, L0_gnn_Wv_w, L0_gnn_Wv_b, L1_gnn_Wqk, L1_gnn_Wv):
    import jax
    import jax.numpy as jnp

    def _L0_gnn_ref(x, adj, Wq_w, Wq_b, Wk_w, Wk_b, Wv_w, Wv_b):
        import jax, jax.numpy as jnp
        import numpy as np
        B, N, D = (8, 1024, 256)
        query = jnp.einsum('bnd,od->bno', x, Wq_w) + Wq_b
        keyt = jnp.einsum('bnd,od->bno', x, Wk_w) + Wk_b
        value = jnp.einsum('bnd,od->bno', x, Wv_w) + Wv_b
        weight = jnp.einsum('bqd,bkd->bqk', query, keyt)
        weight = adj * jnp.exp(weight)
        weight = weight / jnp.sum(weight, axis=2, keepdims=True)
        return jnp.einsum('bqk,bkd->bqd', weight, value)

    def _L1_gnn_ref(X, adj, mask, Wqk, Wv):
        import jax, jax.numpy as jnp
        import numpy as np
        B, N, IN_DIM, ATT_DIM = (2, 4096, 256, 256)
        qk = X @ Wqk
        q, k = jnp.split(qk, 2, axis=-1)
        v = X @ Wv
        att_dim = q.shape[-1]
        inv_scale = 1.0 / jnp.sqrt(jnp.float32(att_dim))
        k_m = k * mask[:, :, None]
        agg = jnp.einsum('bij,bjd->bid', adj, k_m)
        w = inv_scale * mask * jnp.einsum('bid,bid->bi', q, agg)
        L = jax.nn.softmax(w, axis=1)[:, :, None] * v
        return L
    h = jnp.maximum(_layernorm(x, axis=-1), 0.0)
    x = x + _L0_gnn_ref(h, adj, L0_gnn_Wq_w, L0_gnn_Wq_b, L0_gnn_Wk_w, L0_gnn_Wk_b, L0_gnn_Wv_w, L0_gnn_Wv_b)
    h = jnp.maximum(_layernorm(x, axis=-1), 0.0)
    x = x + _L1_gnn_ref(h, adj, nodemask, L1_gnn_Wqk, L1_gnn_Wv)
    return x

_drawn_inputs = setup_inputs


def setup_inputs(seed=0):
    import zlib

    import numpy as np

    out = dict(_drawn_inputs(seed))
    spreads = {'L0_gnn_Wq_b': (0.0, 0.1), 'L0_gnn_Wk_b': (0.0, 0.8), 'L0_gnn_Wv_b': (0.0, 0.1)}
    factors = {'L1_gnn_Wqk': 8.0, 'L1_gnn_Wv': 7.617}
    for name, (base, spread) in spreads.items():
        noise = np.random.default_rng([zlib.crc32(name.encode()), seed]).standard_normal(out[name].shape)
        drawn = base * np.exp(spread * noise) if base else spread * noise
        out[name] = jnp.asarray(drawn.astype(out[name].dtype))
    for name, factor in factors.items():
        out[name] = (out[name] * factor).astype(out[name].dtype)
    return out
```

```python
from contextlib import ExitStack

import concourse.bass as bass
from concourse import mybir

F32 = mybir.dt.float32
F32R = mybir.dt.float32r
ALU = mybir.AluOpType
ACT = mybir.ActivationFunctionType
AX_X = mybir.AxisListType.X

P = 128
LN_EPS = 1e-5


class Batch:

    def __init__(self, number, half, parity):
        self.number, self.half, self.parity = number, half, parity

    def count(self, per_batch, k):
        return self.number * per_batch + k

    def landed(self):
        return (self.half + 1) * 16


def batch(n):
    return Batch(n, n // 2, n % 2)


def graph_layers_kernel(nc, x, adj, nodemask, wq, bq, wk, bk, wvT, bv, wqkT, wv1, out):
    B, N, D = x.shape
    T = N // P
    KD = D // P
    VC = D + 2
    INV_SCALE = 1.0 / float(D) ** 0.5
    assert T == 4 and KD == 2 and N == 512 and D == 256 and B % 2 == 0 and B >= 4

    x_rows = x.rearrange("b (t p) d -> b p t d", p=P)
    adj_rows = adj.rearrange("b (t p) j -> b p t j", p=P)
    out_rows = out.rearrange("b (t p) d -> b p t d", p=P)

    with ExitStack() as ctx:
        def sb(name, shape, dt=F32):
            return ctx.enter_context(nc.sbuf_tensor(name, shape, dt))

        def sem(name):
            return ctx.enter_context(nc.semaphore(name))

        ps = ctx.enter_context(nc.psum_tensor("ps", [P, 8, 512], F32))
        BANK_TR = 0
        BANK_PROJ = 2
        BANK_V = 4
        BANK_S = (4, 5, 7, 5)
        BANK_T = (6, 4, 6, 7)
        BANK_V2 = 4
        small = ps[:, 6, :]

        ident = sb("ident", [P, P])
        ones = sb("ones", [P, P])
        neg_half = sb("neg_half", [P, T])
        wq_sb = sb("wq_sb", [P, KD, D])
        wk_bk = sb("wk_bk", [P, KD, D + 1])
        bq_col = sb("bq_col", [P, KD])
        bqbk_col = sb("bqbk_col", [P, KD])
        wvT_sb = sb("wvT_sb", [P, KD, D])
        wqkT_sb = sb("wqkT_sb", [P, 2 * KD, D])
        wv1_sb = sb("wv1_sb", [P, KD, D])
        mask_rows = sb("mask_rows", [B * T, P])
        mask_scaled = sb("mask_scaled", [P, B * T])
        bv_all = sb("bv_all", [P, D])
        M0h, M0l = sb("M0h", [P, KD, D], F32R), sb("M0l", [P, KD, D], F32R)
        M1h, M1l = sb("M1h", [P, KD, D], F32R), sb("M1l", [P, KD, D], F32R)
        Wvh, Wvl = sb("Wvh", [P, KD, VC], F32R), sb("Wvl", [P, KD, VC], F32R)
        W1h, W1l = sb("W1h", [P, KD, D], F32R), sb("W1l", [P, KD, D], F32R)
        ub = sb("ub", [P, KD])
        bqbk = sb("bqbk", [P, 1])

        x_in = [sb(f"x_in{i}", [P, T, D]) for i in range(2)]
        adj_in = [sb(f"adj_in{i}", [P, T, N]) for i in range(2)]
        mask_all = [sb(f"mask_all{i}", [P, N]) for i in range(2)]
        adj_m = [sb(f"adj_m{i}", [P, T, N]) for i in range(2)]
        x1 = [sb(f"x1_{i}", [P, T, D]) for i in range(2)]
        x_bv = sb("x_bv", [P, T, D])
        xn, xn2 = sb("xn", [P, T, D]), sb("xn2", [P, T, D])
        hTh, hTl = sb("hTh", [P, KD, N], F32R), sb("hTl", [P, KD, N], F32R)
        h2Th, h2Tl = sb("h2Th", [P, KD, N], F32R), sb("h2Tl", [P, KD, N], F32R)
        uTh, uTl = sb("uTh", [P, KD, N], F32R), sb("uTl", [P, KD, N], F32R)
        rTh, rTl = sb("rTh", [P, KD, N], F32R), sb("rTl", [P, KD, N], F32R)
        vh, vl = sb("vh", [P, T, D], F32R), sb("vl", [P, T, D], F32R)
        c_row = sb("c_row", [P, T])
        E = sb("E", [P, T, N])
        Pm = sb("Pm", [P, T, N])
        row_sum, row_inv = sb("row_sum", [P, T]), sb("row_inv", [P, T])
        PTh, PTl = sb("PTh", [P, T, T, P], F32R), sb("PTl", [P, T, T, P], F32R)
        st1, st2 = sb("st1", [P, T, 6]), sb("st2", [P, T, 6])
        mom1, mom2 = sb("mom1", [P, 4, T]), sb("mom2", [P, 4, T])
        ve1, ve2 = sb("ve1", [P, T]), sb("ve2", [P, T])
        rstd1, rstd2 = sb("rstd1", [P, T]), sb("rstd2", [P, T])
        nmr1, nmr2 = sb("nmr1", [P, T]), sb("nmr2", [P, T])
        w_junk = sb("w_junk", [P, T, N])
        w_raw, w_log = sb("w_raw", [P, T]), sb("w_log", [P, T])
        max4, neg_diag = sb("max4", [T, 1]), sb("neg_diag", [T, T])
        neg_max = sb("neg_max", [P, 1])
        w_exp, w_sum, w_inv, soft = sb("w_exp", [P, T]), sb("w_sum", [P, 1]), sb("w_inv", [P, 1]), sb("soft", [P, T])
        sv = sb("sv", [P, T, D])
        y = sb("y", [P, T, D])

        weights_in = sem("weights_in")
        const_ready = sem("const_ready")
        set_psum, set_done, set_chain = sem("set_psum"), sem("set_done"), sem("set_chain")
        x_landed = [sem(f"x_landed{i}") for i in range(2)]
        adj_landed = [sem(f"adj_landed{i}") for i in range(2)]
        mask_landed = [sem(f"mask_landed{i}") for i in range(2)]
        stats1, var1, rstd1_ready, nmr1_ready = sem("stats1"), sem("var1"), sem("rstd1_ready"), sem("nmr1_ready")
        stats2, var2, rstd2_ready, nmr2_ready = sem("stats2"), sem("var2"), sem("rstd2_ready"), sem("nmr2_ready")
        moments1, moments2 = sem("moments1"), sem("moments2")
        xn_ready, xn2_ready = sem("xn_ready"), sem("xn2_ready")
        hT_psum, hTh_ready, hTl_ready = sem("hT_psum"), sem("hTh_ready"), sem("hTl_ready")
        h2T_psum, h2Th_ready, h2Tl_ready = sem("h2T_psum"), sem("h2Th_ready"), sem("h2Tl_ready")
        uT_psum, uTh_ready, uTl_ready = sem("uT_psum"), sem("uTh_ready"), sem("uTl_ready")
        rT_psum, rTh_ready, rTl_ready = sem("rT_psum"), sem("rTh_ready"), sem("rTl_ready")
        v_psum = sem("v_psum")
        vh_ready, vl_ready, c_ready = sem("vh_ready"), sem("vl_ready"), sem("c_ready")
        s_psum, e_ready, p_ready = sem("s_psum"), sem("e_ready"), sem("p_ready")
        pt_psum, pth_ready, ptl_ready = sem("pt_psum"), sem("pth_ready"), sem("ptl_ready")
        pv_psum, inv_ready, x1_ready = sem("pv_psum"), sem("inv_ready"), sem("x1_ready")
        xbv_ready, adjm_ready = sem("xbv_ready"), sem("adjm_ready")
        t_psum, w_ready = sem("t_psum"), sem("w_ready")
        wlog_ready, wlogT_psum, max4_ready, diag_ready = sem("wlog_ready"), sem("wlogT_psum"), sem("max4_ready"), sem("diag_ready")
        max_psum, negmax_ready, wexp_ready, sum_psum = sem("max_psum"), sem("negmax_ready"), sem("wexp_ready"), sem("sum_psum")
        winv_ready, soft_ready = sem("winv_ready"), sem("soft_ready")
        v2_psum, sv_ready, y_ready = sem("v2_psum"), sem("sv_ready"), sem("y_ready")
        y_free = sem("y_free")

        def f32(t):
            return t.bitcast(F32)

        def steps(eng, step):
            step(batch(0), None, batch(1))
            with eng.Fori(0, (B - 2) // 2) as g:
                step(Batch(g * 2 + 1, g, 1), Batch(g * 2, g, 0), Batch(g * 2 + 2, g + 1, 0))
                step(Batch(g * 2 + 2, g + 1, 0), Batch(g * 2 + 1, g, 1), Batch(g * 2 + 3, g + 1, 1))
            step(batch(B - 1), batch(B - 2), None)
            step(None, batch(B - 1), None)

        block = ctx.enter_context(nc.Block())

        @block.sync
        def _(sp):
            def load(m):
                if not isinstance(m.number, int) or m.number >= 2:
                    last = Batch(m.number - 2, None, None)
                    sp.wait_ge(adjm_ready, last.count(4, 4))
                    sp.wait_ge(p_ready, last.count(4, 4))
                sp.dma_start(x_in[m.parity][:], x_rows[m.number]).then_inc(x_landed[m.parity], 16)
                sp.dma_start(mask_all[m.parity][:], nodemask[bass.ds(m.number, 1), :].to_broadcast([P, N])
                             ).then_inc(mask_landed[m.parity], 16)
                sp.dma_start(adj_in[m.parity][:], adj_rows[m.number]).then_inc(adj_landed[m.parity], 16)

            def step(n, b, m):
                if m is not None:
                    load(m)
                if b is not None:
                    sp.wait_ge(y_ready, b.count(4, 4))
                    sp.dma_start(out_rows[b.number], y[:]).then_inc(y_free, 16)

            load(batch(0))
            for dst, src in (
                (wq_sb[:], wq.rearrange("(k p) d -> p k d", p=P)),
                (wk_bk[:, :, 0:D], wk.rearrange("(k p) d -> p k d", p=P)),
                (wvT_sb[:], wvT.rearrange("(k p) d -> p k d", p=P)),
                (wqkT_sb[:], wqkT.rearrange("(k p) d -> p k d", p=P)),
                (wv1_sb[:], wv1.rearrange("(k p) d -> p k d", p=P)),
                (mask_rows[:], nodemask.rearrange("b (t p) -> (b t) p", p=P)),
                (bv_all[:], bv.rearrange("(a d) -> a d", a=1).to_broadcast([P, D])),
            ):
                sp.dma_start(dst, src).then_inc(weights_in, 16)
            for dst, src in (
                (wk_bk[:, :, D:D + 1], bk.rearrange("(k p a) -> p k a", p=P, a=1)),
                (bq_col[:].rearrange("p (k a) -> p k a", a=1), bq.rearrange("(k p a) -> p k a", p=P, a=1)),
            ):
                sp.dma_start(dst, src, allow_slow_non_contiguous=True).then_inc(weights_in, 16)
            steps(sp, step)
            sp.wait_ge(y_free, 16 * (B + 1))

        WEIGHT_LOADS = 9 * 16

        @block.gpsimd
        def _(pool):
            nc.gpsimd.memset(ident[:], 0.0).then_inc(const_ready, 1)
            nc.gpsimd.memset(ones[:], 1.0).then_inc(const_ready, 1)
            nc.gpsimd.memset(neg_half[:], -0.5).then_inc(const_ready, 1)
            pool.wait_ge(const_ready, 3)
            nc.gpsimd.affine_select(out=ident[:], in_=ident[:], compare_op=ALU.not_equal, fill=1.0, base=0,
                                    pattern=[[-1, P]], channel_multiplier=1).then_inc(const_ready, 1)
            pool.sem_inc(y_free, 16)

            def power1(m):
                pool.wait_ge(var1, m.count(1, 1))
                nc.gpsimd.tensor_tensor(rstd1[:], ve1[:], neg_half[:], ALU.pow).then_inc(rstd1_ready, 1)

            def step(n, b, m):
                if n is not None:
                    pool.wait_ge(x_landed[n.parity], n.landed())
                    if b is not None:
                        pool.wait_ge(x1_ready, b.count(4, 4))
                    nc.gpsimd.tensor_tensor(x_bv[:], x_in[n.parity][:],
                                            bv_all[:].rearrange("p (o d) -> p o d", o=1).to_broadcast([P, T, D]),
                                            ALU.add).then_inc(xbv_ready, 1)
                    pool.wait_ge(adj_landed[n.parity], n.landed())
                    pool.wait_ge(mask_landed[n.parity], n.landed())
                    for t in range(T):
                        nc.gpsimd.tensor_tensor(adj_m[n.parity][:, t], adj_in[n.parity][:, t],
                                                mask_all[n.parity][:], ALU.mult).then_inc(adjm_ready, 1)
                if m is not None:
                    power1(m)
                if n is not None:
                    pool.wait_ge(var2, n.count(1, 1))
                    nc.gpsimd.tensor_tensor(rstd2[:], ve2[:], neg_half[:], ALU.pow).then_inc(rstd2_ready, 1)
                if b is not None:
                    pool.wait_ge(y_free, b.count(16, 16))
                    for t in range(T):
                        pool.wait_ge(sv_ready, b.count(4, t + 1))
                        nc.gpsimd.tensor_tensor(y[:, t], sv[:, t], x1[b.parity][:, t], ALU.add).then_inc(y_ready, 1)

            pool.wait_ge(weights_in, WEIGHT_LOADS)
            power1(batch(0))
            steps(pool, step)

        @block.scalar
        def _(act):
            def normalise1(m, t):
                if t == 0:
                    act.wait_ge(nmr1_ready, m.count(1, 1))
                nc.scalar.activation(xn[:, t], x_in[m.parity][:, t], ACT.Identity, bias=nmr1[:, t:t + 1],
                                     scale=rstd1[:, t:t + 1]).then_inc(xn_ready, 1)

            def hT_hi(m):
                for k in range(KD):
                    act.wait_ge(hT_psum, m.count(2, k + 1))
                    nc.scalar.activation(hTh[:, k], ps[:, BANK_TR + k], ACT.Relu).then_inc(hTh_ready, 1)

            def exp_scores(n, t):
                act.wait_ge(s_psum, n.count(4, t + 1))
                act.wait_ge(c_ready, n.count(2, t // 2 + 1))
                nc.scalar.activation(E[:, t], ps[:, BANK_S[t]], ACT.Exp, bias=c_row[:, t:t + 1]
                                     ).then_inc(e_ready, 1)

            def PT_hi(n, t):
                act.wait_ge(pt_psum, n.count(4, t + 1))
                nc.scalar.activation(PTh[:, t].rearrange("p a b -> p (a b)"), ps[:, BANK_TR + t % 2], ACT.Identity
                                     ).then_inc(pth_ready, 1)

            def step(n, b, m):
                if n is not None:
                    for k in range(KD):
                        act.wait_ge(uT_psum, n.count(2, k + 1))
                        nc.scalar.activation(uTh[:, k], ps[:, BANK_PROJ + k], ACT.Identity, bias=ub[:, k:k + 1]
                                             ).then_inc(uTh_ready, 1)
                if b is not None:
                    for k in range(KD):
                        act.wait_ge(h2T_psum, b.count(2, k + 1))
                        nc.scalar.activation(h2Th[:, k], ps[:, BANK_TR + k], ACT.Relu).then_inc(h2Th_ready, 1)
                if n is not None:
                    for k in range(2):
                        act.wait_ge(v_psum, n.count(4, 2 * k + 2))
                        nc.scalar.activation(vh[:, 2 * k:2 * k + 2], ps[:, BANK_V + 2 * k:BANK_V + 2 * k + 2, 0:D],
                                             ACT.Identity).then_inc(vh_ready, 1)
                if b is not None:
                    for k in range(KD):
                        act.wait_ge(rT_psum, b.count(2, k + 1))
                        nc.scalar.activation(rTh[:, k], ps[:, BANK_PROJ + k], ACT.Identity).then_inc(rTh_ready, 1)
                if n is not None:
                    exp_scores(n, 0)
                    exp_scores(n, 1)
                    PT_hi(n, 0)
                    exp_scores(n, 2)
                    PT_hi(n, 1)
                    exp_scores(n, 3)
                    if m is not None:
                        normalise1(m, 0)
                    PT_hi(n, 2)
                    if m is not None:
                        normalise1(m, 1)
                    PT_hi(n, 3)
                if m is not None:
                    normalise1(m, 2)
                    normalise1(m, 3)
                    hT_hi(m)
                if b is not None:
                    act.wait_ge(negmax_ready, b.count(1, 1))
                    nc.scalar.activation(w_exp[:], w_log[:], ACT.Exp, bias=neg_max[:], accum_out=w_sum[:]
                                         ).then_inc(wexp_ready, 1)
                if n is not None:
                    act.wait_ge(nmr2_ready, n.count(1, 1))
                    for t in range(T):
                        nc.scalar.activation(xn2[:, t], x1[n.parity][:, t], ACT.Identity, bias=nmr2[:, t:t + 1],
                                             scale=rstd2[:, t:t + 1]).then_inc(xn2_ready, 1)
                if b is not None:
                    act.wait_ge(v2_psum, b.count(4, 4))
                    act.wait_ge(soft_ready, b.count(1, 1))
                    if n is None:
                        act.wait_ge(y_ready, b.count(4, 0))
                    for t in range(T):
                        v2 = ps[:, BANK_V2 + t // 2, (t % 2) * D:(t % 2 + 1) * D]
                        nc.scalar.activation(sv[:, t], v2, ACT.Copy, scale=soft[:, t:t + 1]).then_inc(sv_ready, 1)

            for t in range(T):
                normalise1(batch(0), t)
            hT_hi(batch(0))
            act.wait_ge(set_done, 1)
            steps(act, step)

        @block.vector
        def _(dve):
            def stats(m, t):
                if t == 0:
                    dve.wait_ge(x_landed[m.parity], m.landed())
                nc.vector.bn_stats(st1[:, t], x_in[m.parity][:, t]).then_inc(stats1, 1)

            def variance(n, st, mom, ve, stats_sem, mom_sem, var_sem):
                dve.wait_ge(stats_sem, n.count(4, 4))
                nc.vector.tensor_tensor(mom[:, 0], st[:, :, 1], st[:, :, 4], ALU.add).then_inc(mom_sem, 1)
                nc.vector.tensor_tensor(mom[:, 1], st[:, :, 1], st[:, :, 4], ALU.subtract).then_inc(mom_sem, 1)
                nc.vector.scalar_tensor_tensor(out=mom[:, 2], in0=st[:, :, 2], scalar=D * LN_EPS, in1=st[:, :, 5],
                                               op0=ALU.add, op1=ALU.add).then_inc(mom_sem, 1)
                dve.wait_ge(mom_sem, n.count(4, 2))
                nc.vector.scalar_tensor_tensor(out=mom[:, 3], in0=mom[:, 1], scalar=0.25, in1=mom[:, 1],
                                               op0=ALU.mult, op1=ALU.mult).then_inc(mom_sem, 1)
                dve.wait_ge(mom_sem, n.count(4, 4))
                nc.vector.scalar_tensor_tensor(out=ve[:], in0=mom[:, 2], scalar=1.0 / D, in1=mom[:, 3],
                                               op0=ALU.mult, op1=ALU.add).then_inc(var_sem, 1)

            def neg_mean_rstd(n, mom, rstd, nmr, rstd_sem, nmr_sem):
                dve.wait_ge(rstd_sem, n.count(1, 1))
                nc.vector.scalar_tensor_tensor(out=nmr[:], in0=mom[:, 0], scalar=-0.5, in1=rstd[:],
                                               op0=ALU.mult, op1=ALU.mult).then_inc(nmr_sem, 1)

            def hT_lo(m):
                for k in range(KD):
                    dve.wait_ge(hTh_ready, m.count(2, k + 1))
                    nc.vector.scalar_tensor_tensor(out=hTl[:, k], in0=ps[:, BANK_TR + k], scalar=0.0,
                                                   in1=f32(hTh[:, k]), op0=ALU.max, op1=ALU.subtract
                                                   ).then_inc(hTl_ready, 1)

            def weigh(n, t):
                dve.wait_ge(e_ready, n.count(4, t + 1))
                if t == 0:
                    dve.wait_ge(adj_landed[n.parity], n.landed())
                nc.vector.tensor_tensor_reduce(out=Pm[:, t], in0=E[:, t], in1=adj_in[n.parity][:, t], scale=1.0,
                                               scalar=0.0, op0=ALU.mult, op1=ALU.add,
                                               accum_out=row_sum[:, t:t + 1]).then_inc(p_ready, 1)

            def PT_lo(n, t):
                dve.wait_ge(pth_ready, n.count(4, t + 1))
                nc.vector.tensor_tensor(PTl[:, t].rearrange("p a b -> p (a b)"), ps[:, BANK_TR + t % 2],
                                        f32(PTh[:, t].rearrange("p a b -> p (a b)")), ALU.subtract
                                        ).then_inc(ptl_ready, 1)

            def invert(n, t):
                dve.wait_ge(p_ready, n.count(4, t + 1))
                nc.vector.reciprocal(row_inv[:, t:t + 1], row_sum[:, t:t + 1]).then_inc(inv_ready, 1)

            def residual(n, t):
                dve.wait_ge(pv_psum, n.count(4, t + 1))
                dve.wait_ge(inv_ready, n.count(4, t + 1))
                if t == 0:
                    dve.wait_ge(xbv_ready, n.count(1, 1))
                nc.vector.scalar_tensor_tensor(out=x1[n.parity][:, t], in0=ps[:, BANK_PROJ + t % 2, 0:D],
                                               scalar=row_inv[:, t:t + 1], in1=x_bv[:, t],
                                               op0=ALU.mult, op1=ALU.add).then_inc(x1_ready, 1)

            def stats_x1(n, t):
                dve.wait_ge(x1_ready, n.count(4, t + 1))
                nc.vector.bn_stats(st2[:, t], x1[n.parity][:, t]).then_inc(stats2, 1)

            def row_score(b, t):
                dve.wait_ge(t_psum, b.count(4, t + 1))
                if t == 0:
                    dve.wait_ge(adjm_ready, b.count(4, 4))
                nc.vector.tensor_tensor_reduce(out=w_junk[:, t], in0=ps[:, BANK_T[t]], in1=adj_m[b.parity][:, t],
                                               scale=1.0, scalar=0.0, op0=ALU.mult, op1=ALU.add,
                                               accum_out=w_raw[:, t:t + 1]).then_inc(w_ready, 1)

            def step(n, b, m):
                if n is not None:
                    for k in range(KD):
                        dve.wait_ge(uTh_ready, n.count(2, k + 1))
                        nc.vector.scalar_tensor_tensor(out=uTl[:, k], in0=ps[:, BANK_PROJ + k], scalar=ub[:, k:k + 1],
                                                       in1=f32(uTh[:, k]), op0=ALU.add, op1=ALU.subtract
                                                       ).then_inc(uTl_ready, 1)
                if b is not None:
                    for k in range(KD):
                        dve.wait_ge(h2Th_ready, b.count(2, k + 1))
                        nc.vector.scalar_tensor_tensor(out=h2Tl[:, k], in0=ps[:, BANK_TR + k], scalar=0.0,
                                                       in1=f32(h2Th[:, k]), op0=ALU.max, op1=ALU.subtract
                                                       ).then_inc(h2Tl_ready, 1)
                if n is not None:
                    for k in range(2):
                        pair = slice(2 * k, 2 * k + 2)
                        banks = slice(BANK_V + 2 * k, BANK_V + 2 * k + 2)
                        dve.wait_ge(vh_ready, n.count(2, k + 1))
                        nc.vector.tensor_tensor(vl[:, pair], ps[:, banks, 0:D], f32(vh[:, pair]), ALU.subtract
                                                ).then_inc(vl_ready, 1)
                        nc.vector.tensor_scalar(c_row[:, pair], ps[:, banks, D], bqbk[:], None, ALU.add
                                                ).then_inc(c_ready, 1)
                if b is not None:
                    for k in range(KD):
                        dve.wait_ge(rTh_ready, b.count(2, k + 1))
                        nc.vector.tensor_tensor(rTl[:, k], ps[:, BANK_PROJ + k], f32(rTh[:, k]), ALU.subtract
                                                ).then_inc(rTl_ready, 1)
                if m is not None:
                    stats(m, 0)
                    stats(m, 1)
                if n is not None:
                    weigh(n, 0)
                    if m is not None:
                        stats(m, 2)
                    weigh(n, 1)
                if m is not None:
                    stats(m, 3)
                    variance(m, st1, mom1, ve1, stats1, moments1, var1)
                if b is not None:
                    row_score(b, 0)
                if n is not None:
                    PT_lo(n, 0)
                    invert(n, 0)
                    weigh(n, 2)
                    PT_lo(n, 1)
                    invert(n, 1)
                if m is not None:
                    neg_mean_rstd(m, mom1, rstd1, nmr1, rstd1_ready, nmr1_ready)
                if b is not None:
                    row_score(b, 1)
                if n is not None:
                    residual(n, 0)
                    weigh(n, 3)
                    stats_x1(n, 0)
                    PT_lo(n, 2)
                    invert(n, 2)
                if b is not None:
                    row_score(b, 2)
                if n is not None:
                    residual(n, 1)
                    stats_x1(n, 1)
                    PT_lo(n, 3)
                    invert(n, 3)
                if b is not None:
                    row_score(b, 3)
                    dve.wait_ge(w_ready, b.count(4, 4))
                    nc.vector.tensor_tensor(w_log[:], w_raw[:], mask_scaled[:, bass.ds(b.number * T, T)],
                                            ALU.mult).then_inc(wlog_ready, 1)
                if n is not None:
                    residual(n, 2)
                    stats_x1(n, 2)
                if b is not None:
                    dve.wait_ge(wlogT_psum, b.count(1, 1))
                    nc.vector.tensor_reduce(max4[:], small[0:T, 0:P], AX_X, ALU.max).then_inc(max4_ready, 1)
                    dve.wait_ge(max4_ready, b.count(1, 1))
                    nc.vector.tensor_scalar(neg_diag[:], ident[0:T, 0:T], max4[:], -1.0, ALU.mult, ALU.mult
                                            ).then_inc(diag_ready, 1)
                if n is not None:
                    residual(n, 3)
                    stats_x1(n, 3)
                    variance(n, st2, mom2, ve2, stats2, moments2, var2)
                if b is not None:
                    dve.wait_ge(max_psum, b.count(1, 1))
                    nc.vector.tensor_reduce(neg_max[:], small[:, P:P + T], AX_X, ALU.min).then_inc(negmax_ready, 1)
                if m is not None:
                    hT_lo(m)
                if n is not None:
                    neg_mean_rstd(n, mom2, rstd2, nmr2, rstd2_ready, nmr2_ready)
                if b is not None:
                    dve.wait_ge(sum_psum, b.count(1, 1))
                    nc.vector.reciprocal(w_inv[:], small[:, 2 * P:2 * P + 1]).then_inc(winv_ready, 1)
                    dve.wait_ge(winv_ready, b.count(1, 1))
                    nc.vector.tensor_scalar(soft[:], w_exp[:], w_inv[:], None, ALU.mult).then_inc(soft_ready, 1)

            first = batch(0)
            for t in range(T):
                stats(first, t)
            variance(first, st1, mom1, ve1, stats1, moments1, var1)
            neg_mean_rstd(first, mom1, rstd1, nmr1, rstd1_ready, nmr1_ready)

            chain = [0]

            def link(ins):
                chain[0] += 1
                ins.then_inc(set_chain, 1)
                dve.wait_ge(set_chain, chain[0])

            dve.wait_ge(weights_in, WEIGHT_LOADS)
            link(nc.vector.tensor_tensor(bqbk_col[:], bq_col[:], wk_bk[:, :, D], ALU.mult))
            link(nc.vector.tensor_copy(Wvh[:, :, 0:D], wvT_sb[:]))
            nc.vector.tensor_tensor(Wvl[:, :, 0:D], wvT_sb[:], f32(Wvh[:, :, 0:D]), ALU.subtract)
            link(nc.vector.tensor_copy(W1h[:], wv1_sb[:]))
            nc.vector.tensor_tensor(W1l[:], wv1_sb[:], f32(W1h[:]), ALU.subtract)
            nc.vector.memset(Wvl[:, :, D:VC].bitcast(F32), 0.0)
            link(nc.vector.memset(Wvh[:, :, D:VC].bitcast(F32), 0.0))
            dve.wait_ge(set_psum, 1)
            link(nc.vector.tensor_copy(M0h[:], ps[:, 0:2, 0:D]))
            nc.vector.tensor_tensor(M0l[:], ps[:, 0:2, 0:D], f32(M0h[:]), ALU.subtract)
            link(nc.vector.tensor_copy(M1h[:], ps[:, 2:4, 0:D]))
            nc.vector.tensor_tensor(M1l[:], ps[:, 2:4, 0:D], f32(M1h[:]), ALU.subtract)
            link(nc.vector.tensor_copy(Wvh[:, :, D], ps[:, 0:2, D]))
            nc.vector.tensor_tensor(Wvl[:, :, D], ps[:, 0:2, D], f32(Wvh[:, :, D]), ALU.subtract)
            nc.vector.tensor_copy(ub[:], ps[:, 4, 0:KD])
            nc.vector.tensor_copy(bqbk[:], ps[:, 5, 0:1])
            nc.vector.tensor_scalar(mask_scaled[:], ps[:, 6, 0:B * T], INV_SCALE, None, ALU.mult).then_inc(set_done, 1)
            hT_lo(first)
            steps(dve, step)

        @block.tensor
        def _(pe):
            def product(out_ap, pairs, done=None):
                last = 3 * len(pairs) - 1
                i = 0
                for (ah, al), (bh, bl) in pairs:
                    for a, b_ in ((ah, bh), (ah, bl), (al, bh)):
                        mm = nc.tensor.matmul(out_ap, a, b_, start=(i == 0), stop=(i == last))
                        i += 1
                if done is not None:
                    mm.then_inc(done, 1)

            def transposed_rows(src, done):
                for k in range(KD):
                    for t in range(T):
                        mm = nc.tensor.transpose(ps[:, BANK_TR + k, t * P:(t + 1) * P],
                                                 src[:, t, k * P:(k + 1) * P], ident[:])
                    mm.then_inc(done, 1)

            def TX(m):
                pe.wait_ge(xn_ready, m.count(4, 4))
                transposed_rows(xn, hT_psum)

            def project(wh, wl, inh, inl, done):
                for k in range(KD):
                    product(ps[:, BANK_PROJ + k],
                            [((wh[:, q, k * P:(k + 1) * P], wl[:, q, k * P:(k + 1) * P]), (inh[:, q], inl[:, q]))
                             for q in range(KD)], done)

            def scores(ah, al, bh, bl, t, bank, done):
                product(ps[:, bank],
                        [((ah[:, q, t * P:(t + 1) * P], al[:, q, t * P:(t + 1) * P]), (bh[:, q], bl[:, q]))
                         for q in range(KD)], done)

            def S(n, t):
                if t == 0:
                    pe.wait_ge(vl_ready, n.count(2, 1))
                    pe.wait_ge(c_ready, n.count(2, 1))
                    pe.wait_ge(uTl_ready, n.count(2, 2))
                if t == 2:
                    pe.wait_ge(c_ready, n.count(2, 2))
                if t == 3:
                    pe.wait_ge(e_ready, n.count(4, 2))
                scores(uTh, uTl, hTh, hTl, t, BANK_S[t], s_psum)

            def Tm(n, b, t):
                if t == 0:
                    pe.wait_ge(rTl_ready, b.count(2, 2))
                    if n is not None:
                        pe.wait_ge(c_ready, n.count(2, 2))
                if t == 1:
                    if n is not None:
                        pe.wait_ge(e_ready, n.count(4, 1))
                    else:
                        pe.wait_ge(sv_ready, b.count(4, 0))
                if t == 2:
                    pe.wait_ge(w_ready, b.count(4, 1))
                if t == 3 and n is not None:
                    pe.wait_ge(e_ready, n.count(4, 3))
                scores(rTh, rTl, h2Th, h2Tl, t, BANK_T[t], t_psum)

            def TP(n, t):
                pe.wait_ge(p_ready, n.count(4, t + 1))
                if t >= 2:
                    pe.wait_ge(ptl_ready, n.count(4, t - 1))
                for j in range(T):
                    mm = nc.tensor.transpose(ps[:, BANK_TR + t % 2, j * P:(j + 1) * P],
                                             Pm[:, t, j * P:(j + 1) * P], ident[:])
                mm.then_inc(pt_psum, 1)

            def PV(n, t):
                pe.wait_ge(ptl_ready, n.count(4, t + 1))
                if t == 0:
                    pe.wait_ge(vl_ready, n.count(2, 2))
                if t >= 2:
                    pe.wait_ge(x1_ready, n.count(4, t - 1))
                product(ps[:, BANK_PROJ + t % 2, 0:D],
                        [((PTh[:, t, j], PTl[:, t, j]), (vh[:, j], vl[:, j])) for j in range(T)], pv_psum)

            def step(n, b, m):
                if n is not None:
                    pe.wait_ge(hTl_ready, n.count(2, 2))
                    if b is not None:
                        pe.wait_ge(x1_ready, b.count(4, 4))
                    project(M0h, M0l, hTh, hTl, uT_psum)
                if b is not None:
                    pe.wait_ge(xn2_ready, b.count(4, 4))
                    transposed_rows(xn2, h2T_psum)
                if n is not None:
                    pe.wait_ge(uTh_ready, n.count(2, 1))
                    for t in range(T):
                        product(ps[:, BANK_V + t, 0:VC],
                                [((hTh[:, q, t * P:(t + 1) * P], hTl[:, q, t * P:(t + 1) * P]), (Wvh[:, q], Wvl[:, q]))
                                 for q in range(KD)], v_psum)
                if b is not None:
                    pe.wait_ge(h2Tl_ready, b.count(2, 2))
                    if n is not None:
                        pe.wait_ge(uTl_ready, n.count(2, 2))
                    project(M1h, M1l, h2Th, h2Tl, rT_psum)
                if n is not None:
                    S(n, 0)
                    S(n, 1)
                if b is not None:
                    Tm(n, b, 0)
                if n is not None:
                    TP(n, 0)
                    S(n, 2)
                    TP(n, 1)
                if b is not None:
                    Tm(n, b, 1)
                if n is not None:
                    PV(n, 0)
                    S(n, 3)
                    TP(n, 2)
                if b is not None:
                    Tm(n, b, 2)
                if n is not None:
                    PV(n, 1)
                    TP(n, 3)
                if b is not None:
                    Tm(n, b, 3)
                if n is not None:
                    PV(n, 2)
                if b is not None:
                    pe.wait_ge(wlog_ready, b.count(1, 1))
                    nc.tensor.matmul(small[0:T, 0:P], w_log[:], ident[:], start=True, stop=True).then_inc(wlogT_psum, 1)
                if n is not None:
                    PV(n, 3)
                if m is not None:
                    TX(m)
                if b is not None:
                    pe.wait_ge(diag_ready, b.count(1, 1))
                    nc.tensor.matmul(small[:, P:P + T], ones[0:T, :], neg_diag[:], start=True, stop=True
                                     ).then_inc(max_psum, 1)
                    if n is not None:
                        pe.wait_ge(e_ready, n.count(4, 4))
                    for t in range(T):
                        product(ps[:, BANK_V2 + t // 2, (t % 2) * D:(t % 2 + 1) * D],
                                [((h2Th[:, q, t * P:(t + 1) * P], h2Tl[:, q, t * P:(t + 1) * P]), (W1h[:, q], W1l[:, q]))
                                 for q in range(KD)], v2_psum)
                    pe.wait_ge(wexp_ready, b.count(1, 1))
                    nc.tensor.matmul(small[:, 2 * P:2 * P + 1], ones[:], w_sum[:], start=True, stop=True
                                     ).then_inc(sum_psum, 1)

            pe.wait_ge(const_ready, 4)
            pe.wait_ge(weights_in, WEIGHT_LOADS)
            for k in range(KD):
                for q in range(KD):
                    nc.tensor.matmul(ps[:, k, 0:D + 1], wq_sb[:, q, k * P:(k + 1) * P], wk_bk[:, q],
                                     start=(q == 0), stop=(q == KD - 1))
            for k in range(KD):
                for q in range(KD):
                    nc.tensor.matmul(ps[:, 2 + k, 0:D], wqkT_sb[:, q, k * P:(k + 1) * P], wqkT_sb[:, KD + q],
                                     start=(q == 0), stop=(q == KD - 1))
            for k in range(KD):
                for q in range(KD):
                    nc.tensor.matmul(ps[:, 4, k:k + 1], wk_bk[:, q, k * P:(k + 1) * P], bq_col[:, q:q + 1],
                                     start=(q == 0), stop=(q == KD - 1))
            pe.wait_ge(set_chain, 1)
            for q in range(KD):
                nc.tensor.matmul(ps[:, 5, 0:1], ones[:], bqbk_col[:, q:q + 1], start=(q == 0), stop=(q == KD - 1))
            nc.tensor.transpose(ps[:, 6, 0:B * T], mask_rows[:], ident[0:B * T, 0:B * T]).then_inc(set_psum, 1)
            pe.wait_ge(set_done, 1)
            TX(batch(0))
            steps(pe, step)


def kernel(x, adj, nodemask, L0_gnn_Wq_w, L0_gnn_Wq_b, L0_gnn_Wk_w, L0_gnn_Wk_b, L0_gnn_Wv_w, L0_gnn_Wv_b,
           L1_gnn_Wqk, L1_gnn_Wv):
    import numpy as np
    import concourse.bacc as bacc
    from concourse.bass_utils import run_bass_kernel_spmd

    arrays = {
        "x": x, "adj": adj, "nodemask": nodemask,
        "wq": L0_gnn_Wq_w, "bq": L0_gnn_Wq_b, "wk": L0_gnn_Wk_w, "bk": L0_gnn_Wk_b,
        "wvT": np.transpose(L0_gnn_Wv_w), "bv": L0_gnn_Wv_b,
        "wqkT": np.transpose(L1_gnn_Wqk), "wv1": L1_gnn_Wv,
    }
    arrays = {name: np.ascontiguousarray(a) for name, a in arrays.items()}
    nc = bacc.Bacc("TRN2", target_bir_lowering=False, num_devices=1)
    ins = [nc.dram_tensor(name, a.shape, F32, kind="ExternalInput").ap() for name, a in arrays.items()]
    out = nc.dram_tensor("out", x.shape, F32, kind="ExternalOutput").ap()
    graph_layers_kernel(nc, *ins, out)
    result = run_bass_kernel_spmd(nc, [arrays], core_ids=[0])
    return result.results[0]["out"]
```

```python
from contextlib import ExitStack

import concourse.bass as bass
from concourse import mybir

F32 = mybir.dt.float32
F32R = mybir.dt.float32r
ALU = mybir.AluOpType
ACT = mybir.ActivationFunctionType
AX_X = mybir.AxisListType.X

P = 128
LN_EPS = 1e-5


class Batch:

    def __init__(self, number, half, parity):
        self.number, self.half, self.parity = number, half, parity

    def count(self, per_batch, k):
        return self.number * per_batch + k

    def landed(self):
        return (self.half + 1) * 16


def batch(n):
    return Batch(n, n // 2, n % 2)


def graph_layers_kernel(nc, x, adj, adjT, nodemask, wq, bq, wk, bk, wvT, bv, wqkT, wv1, out):
    B, N, D = x.shape
    T = N // P
    KD = D // P
    VC = D + 2
    INV_SCALE = 1.0 / float(D) ** 0.5
    assert T == 4 and KD == 2 and N == 512 and D == 256 and B % 2 == 0 and B >= 4

    x_rows = x.rearrange("b (t p) d -> b p t d", p=P)
    adj_rows = adj.rearrange("b (t p) j -> b p t j", p=P)
    adjT_rows = adjT.rearrange("b (t p) i -> b p t i", p=P)
    out_rows = out.rearrange("b (t p) d -> b p t d", p=P)

    with ExitStack() as ctx:
        def sb(name, shape, dt=F32):
            return ctx.enter_context(nc.sbuf_tensor(name, shape, dt))

        def sem(name):
            return ctx.enter_context(nc.semaphore(name))

        ps = ctx.enter_context(nc.psum_tensor("ps", [P, 8, 512], F32))
        BANK_TR = 0
        BANK_PROJ = 2
        BANK_V = 4
        BANK_S = (4, 5, 6, 7)
        BANK_T_LAST = (6, 7, 6, 7)
        BANK_V2 = 4
        small = ps[:, 6, :]
        MAX_COL, SUM_COL = P, P + 8

        ident = sb("ident", [P, P])
        ones = sb("ones", [P, P])
        neg_half = sb("neg_half", [P, T])
        wk_sb = sb("wk_sb", [P, KD, D])
        wq_bq = sb("wq_bq", [P, KD, D + 1])
        bk_col = sb("bk_col", [P, KD])
        bqbk_col = sb("bqbk_col", [P, KD])
        wvT_sb = sb("wvT_sb", [P, KD, D])
        wqkT_sb = sb("wqkT_sb", [P, 2 * KD, D])
        wv1_sb = sb("wv1_sb", [P, KD, D])
        mask_rows = sb("mask_rows", [B * T, P])
        mask_scaled = sb("mask_scaled", [P, B * T])
        bv_all = sb("bv_all", [P, D])
        M0h, M0l = sb("M0h", [P, KD, D], F32R), sb("M0l", [P, KD, D], F32R)
        M1h, M1l = sb("M1h", [P, KD, D], F32R), sb("M1l", [P, KD, D], F32R)
        Wvh, Wvl = sb("Wvh", [P, KD, VC], F32R), sb("Wvl", [P, KD, VC], F32R)
        W1h, W1l = sb("W1h", [P, KD, D], F32R), sb("W1l", [P, KD, D], F32R)
        sbias = sb("sbias", [P, KD])
        bqbk = sb("bqbk", [P, 1])

        x_in = [sb(f"x_in{i}", [P, T, D]) for i in range(2)]
        adjT_in = [sb(f"adjT_in{i}", [P, T, N]) for i in range(2)]
        adj_in = [sb(f"adj_in{i}", [P, T, N]) for i in range(2)]
        mask_all = [sb(f"mask_all{i}", [P, N]) for i in range(2)]
        x1 = [sb(f"x1_{i}", [P, T, D]) for i in range(2)]
        x_bv = sb("x_bv", [P, T, D])
        xn, xn2 = sb("xn", [P, T, D]), sb("xn2", [P, T, D])
        hTh, hTl = sb("hTh", [P, KD, N], F32R), sb("hTl", [P, KD, N], F32R)
        h2Th, h2Tl = sb("h2Th", [P, KD, N], F32R), sb("h2Tl", [P, KD, N], F32R)
        sTh, sTl = sb("sTh", [P, KD, N], F32R), sb("sTl", [P, KD, N], F32R)
        s2Th, s2Tl = sb("s2Th", [P, KD, N], F32R), sb("s2Tl", [P, KD, N], F32R)
        vh, vl = sb("vh", [P, T, VC], F32R), sb("vl", [P, T, VC], F32R)
        e_row = sb("e_row", [P, T])
        E = sb("E", [P, T, N])
        Pm = sb("Pm", [P, T, N])
        Ph, Pl = sb("Ph", [P, T, N], F32R), sb("Pl", [P, T, N], F32R)
        row_inv = sb("row_inv", [P, T])
        st1, st2 = sb("st1", [P, T, 6]), sb("st2", [P, T, 6])
        mom1, mom2 = sb("mom1", [P, 4, T]), sb("mom2", [P, 4, T])
        ve1, ve2 = sb("ve1", [P, T]), sb("ve2", [P, T])
        rstd1, rstd2 = sb("rstd1", [P, T]), sb("rstd2", [P, T])
        nmr1, nmr2 = sb("nmr1", [P, T]), sb("nmr2", [P, T])
        w_junk = sb("w_junk", [P, T, N])
        w_raw, w_log = sb("w_raw", [P, T]), sb("w_log", [P, T])
        max4, neg_diag = sb("max4", [T, 1]), sb("neg_diag", [T, T])
        neg_max = sb("neg_max", [P, 1])
        w_exp, w_sum, w_inv, soft = sb("w_exp", [P, T]), sb("w_sum", [P, 1]), sb("w_inv", [P, 1]), sb("soft", [P, T])
        sv = sb("sv", [P, T, D])
        y = sb("y", [P, T, D])

        w0_landed, wv_landed, late_landed = sem("w0_landed"), sem("wv_landed"), sem("late_landed")
        v_ones, m1_psum, m1_ready = sem("v_ones"), sem("m1_psum"), sem("m1_ready")
        const_ready = sem("const_ready")
        bqbk_ready, set_psum, set_done, set_chain = sem("bqbk_ready"), sem("set_psum"), sem("set_done"), sem("set_chain")
        x_landed = [sem(f"x_landed{i}") for i in range(2)]
        adjT_landed = [sem(f"adjT_landed{i}") for i in range(2)]
        adj_landed = [sem(f"adj_landed{i}") for i in range(2)]
        mask_landed = [sem(f"mask_landed{i}") for i in range(2)]
        stats1, var1, rstd1_ready, nmr1_ready = sem("stats1"), sem("var1"), sem("rstd1_ready"), sem("nmr1_ready")
        stats2, var2, rstd2_ready, nmr2_ready = sem("stats2"), sem("var2"), sem("rstd2_ready"), sem("nmr2_ready")
        moments1, moments2 = sem("moments1"), sem("moments2")
        xn_ready, xn2_ready = sem("xn_ready"), sem("xn2_ready")
        hT_psum, hTh_ready, hTl_ready = sem("hT_psum"), sem("hTh_ready"), sem("hTl_ready")
        h2T_psum, h2Th_ready, h2Tl_ready = sem("h2T_psum"), sem("h2Th_ready"), sem("h2Tl_ready")
        sT_psum, sTh_ready, sTl_ready = sem("sT_psum"), sem("sTh_ready"), sem("sTl_ready")
        s2T_psum, s2Th_ready, s2Tl_ready = sem("s2T_psum"), sem("s2Th_ready"), sem("s2Tl_ready")
        v_psum = sem("v_psum")
        vh_ready, vl_ready, e_ready = sem("vh_ready"), sem("vl_ready"), sem("e_ready")
        s_psum, exp_ready, p_ready = sem("s_psum"), sem("exp_ready"), sem("p_ready")
        ph_ready, pl_ready = sem("ph_ready"), sem("pl_ready")
        pv_psum, inv_ready, x1_ready = sem("pv_psum"), sem("inv_ready"), sem("x1_ready")
        xbv_ready, adjm_ready = sem("xbv_ready"), sem("adjm_ready")
        t_psum, w_ready = sem("t_psum"), sem("w_ready")
        wlog_ready, wlogT_psum, max4_ready, diag_ready = sem("wlog_ready"), sem("wlogT_psum"), sem("max4_ready"), sem("diag_ready")
        max_psum, negmax_ready, wexp_ready, sum_psum = sem("max_psum"), sem("negmax_ready"), sem("wexp_ready"), sem("sum_psum")
        winv_ready, soft_ready = sem("winv_ready"), sem("soft_ready")
        v2_psum, sv_ready, y_ready = sem("v2_psum"), sem("sv_ready"), sem("y_ready")
        y_free = sem("y_free")

        def f32(t):
            return t.bitcast(F32)

        def steps(eng, step):
            step(batch(0), None, batch(1))
            with eng.Fori(0, (B - 2) // 2) as g:
                step(Batch(g * 2 + 1, g, 1), Batch(g * 2, g, 0), Batch(g * 2 + 2, g + 1, 0))
                step(Batch(g * 2 + 2, g + 1, 0), Batch(g * 2 + 1, g, 1), Batch(g * 2 + 3, g + 1, 1))
            step(batch(B - 1), batch(B - 2), None)
            step(None, batch(B - 1), None)

        W0_LOADS, WV_LOADS, LATE_LOADS = 4 * 16, 16, 4 * 16
        block = ctx.enter_context(nc.Block())

        @block.sync
        def _(sp):
            def load_x(m):
                sp.dma_start(x_in[m.parity][:], x_rows[m.number]).then_inc(x_landed[m.parity], 16)

            def load_adjT(m):
                sp.dma_start(adjT_in[m.parity][:], adjT_rows[m.number]).then_inc(adjT_landed[m.parity], 16)

            def load_adj(m):
                sp.dma_start(mask_all[m.parity][:], nodemask[bass.ds(m.number, 1), :].to_broadcast([P, N])
                             ).then_inc(mask_landed[m.parity], 16)
                sp.dma_start(adj_in[m.parity][:], adj_rows[m.number]).then_inc(adj_landed[m.parity], 16)

            def step(n, b, m):
                if m is not None:
                    if b is not None:
                        sp.wait_ge(x1_ready, b.count(4, 4))
                    load_x(m)
                    load_adjT(m)
                    if b is not None:
                        sp.wait_ge(w_ready, b.count(4, 4))
                    load_adj(m)
                if b is not None:
                    if n is None:
                        for t in range(T):
                            sp.wait_ge(y_ready, b.count(4, t + 1))
                            sp.dma_start(out_rows[b.number, :, t], y[:, t]).then_inc(y_free, 16)
                    else:
                        sp.wait_ge(y_ready, b.count(4, 4))
                        sp.dma_start(out_rows[b.number], y[:]).then_inc(y_free, 16)

            def load_weights(*pairs, landed, **how):
                for dst, src in pairs:
                    sp.dma_start(dst, src, **how).then_inc(landed, 16)

            load_x(batch(0))
            load_weights((wk_sb[:], wk.rearrange("(k p) d -> p k d", p=P)),
                         (wq_bq[:, :, 0:D], wq.rearrange("(k p) d -> p k d", p=P)), landed=w0_landed)
            load_weights((wq_bq[:, :, D:D + 1], bq.rearrange("(k p a) -> p k a", p=P, a=1)),
                         (bk_col[:].rearrange("p (k a) -> p k a", a=1), bk.rearrange("(k p a) -> p k a", p=P, a=1)),
                         landed=w0_landed, allow_slow_non_contiguous=True)
            load_weights((wvT_sb[:], wvT.rearrange("(k p) d -> p k d", p=P)), landed=wv_landed)
            load_adjT(batch(0))
            load_weights((bv_all[:], bv.rearrange("(a d) -> a d", a=1).to_broadcast([P, D])),
                         (mask_rows[:], nodemask.rearrange("b (t p) -> (b t) p", p=P)),
                         (wqkT_sb[:], wqkT.rearrange("(k p) d -> p k d", p=P)),
                         (wv1_sb[:], wv1.rearrange("(k p) d -> p k d", p=P)), landed=late_landed)
            load_adj(batch(0))
            steps(sp, step)
            sp.wait_ge(y_free, 16 * (B + T))

        @block.gpsimd
        def _(pool):
            nc.gpsimd.memset(ident[:], 0.0).then_inc(const_ready, 1)
            nc.gpsimd.memset(ones[:], 1.0).then_inc(const_ready, 1)
            nc.gpsimd.memset(neg_half[:], -0.5).then_inc(const_ready, 1)
            pool.wait_ge(const_ready, 3)
            nc.gpsimd.affine_select(out=ident[:], in_=ident[:], compare_op=ALU.not_equal, fill=1.0, base=0,
                                    pattern=[[-1, P]], channel_multiplier=1).then_inc(const_ready, 1)
            pool.sem_inc(y_free, 16)

            def power1(m):
                pool.wait_ge(var1, m.count(1, 1))
                nc.gpsimd.tensor_tensor(rstd1[:], ve1[:], neg_half[:], ALU.pow).then_inc(rstd1_ready, 1)

            def adj_mask(n, t):
                adj_t = adj_in[n.parity][:, t]
                nc.gpsimd.tensor_tensor(adj_t, adj_t, mask_all[n.parity][:], ALU.mult).then_inc(adjm_ready, 1)

            def step(n, b, m):
                if n is not None:
                    if b is not None:
                        pool.wait_ge(x1_ready, b.count(4, 4))
                    pool.wait_ge(x_landed[n.parity], n.landed())
                    nc.gpsimd.tensor_tensor(x_bv[:], x_in[n.parity][:],
                                            bv_all[:].rearrange("p (o d) -> p o d", o=1).to_broadcast([P, T, D]),
                                            ALU.add).then_inc(xbv_ready, 1)
                if n is not None:
                    pool.wait_ge(adj_landed[n.parity], n.landed())
                    pool.wait_ge(mask_landed[n.parity], n.landed())
                    adj_mask(n, 0)
                    adj_mask(n, 1)
                if m is not None:
                    power1(m)
                if n is not None:
                    adj_mask(n, 2)
                    adj_mask(n, 3)
                if n is not None:
                    pool.wait_ge(var2, n.count(1, 1))
                    nc.gpsimd.tensor_tensor(rstd2[:], ve2[:], neg_half[:], ALU.pow).then_inc(rstd2_ready, 1)
                if b is not None and n is not None:
                    pool.wait_ge(y_free, b.count(16, 16))
                    for t in range(T):
                        pool.wait_ge(sv_ready, b.count(4, t + 1))
                        nc.gpsimd.tensor_tensor(y[:, t], sv[:, t], x1[b.parity][:, t], ALU.add).then_inc(y_ready, 1)

            power1(batch(0))
            pool.wait_ge(late_landed, LATE_LOADS)
            steps(pool, step)

        @block.scalar
        def _(act):
            def normalise1(m, t):
                if t == 0:
                    act.wait_ge(nmr1_ready, m.count(1, 1))
                nc.scalar.activation(xn[:, t], x_in[m.parity][:, t], ACT.Identity, bias=nmr1[:, t:t + 1],
                                     scale=rstd1[:, t:t + 1]).then_inc(xn_ready, 1)

            def hT_hi(m):
                for k in range(KD):
                    act.wait_ge(hT_psum, m.count(2, k + 1))
                    nc.scalar.activation(hTh[:, k], ps[:, BANK_TR + k], ACT.Relu).then_inc(hTh_ready, 1)

            def exp_scores(n, t):
                act.wait_ge(s_psum, n.count(4, t + 1))
                act.wait_ge(e_ready, n.count(2, t // 2 + 1))
                nc.scalar.activation(E[:, t], ps[:, BANK_S[t]], ACT.Exp, bias=e_row[:, t:t + 1]
                                     ).then_inc(exp_ready, 1)

            def P_hi(n, t):
                act.wait_ge(p_ready, n.count(4, t + 1))
                nc.scalar.activation(Ph[:, t], Pm[:, t], ACT.Identity).then_inc(ph_ready, 1)

            def step(n, b, m):
                if n is not None:
                    for k in range(KD):
                        act.wait_ge(sT_psum, n.count(2, k + 1))
                        nc.scalar.activation(sTh[:, k], ps[:, BANK_PROJ + k], ACT.Identity, bias=sbias[:, k:k + 1]
                                             ).then_inc(sTh_ready, 1)
                if b is not None:
                    for k in range(KD):
                        act.wait_ge(h2T_psum, b.count(2, k + 1))
                        nc.scalar.activation(h2Th[:, k], ps[:, BANK_TR + k], ACT.Relu).then_inc(h2Th_ready, 1)
                if n is not None:
                    for k in range(2):
                        act.wait_ge(v_psum, n.count(4, 2 * k + 2))
                        nc.scalar.activation(vh[:, 2 * k:2 * k + 2, 0:D], ps[:, BANK_V + 2 * k:BANK_V + 2 * k + 2, 0:D],
                                             ACT.Identity).then_inc(vh_ready, 1)
                if b is not None:
                    for k in range(KD):
                        act.wait_ge(s2T_psum, b.count(2, k + 1))
                        nc.scalar.activation(s2Th[:, k], ps[:, BANK_PROJ + k], ACT.Identity).then_inc(s2Th_ready, 1)
                if n is not None:
                    exp_scores(n, 0)
                    exp_scores(n, 1)
                    P_hi(n, 0)
                    exp_scores(n, 2)
                    P_hi(n, 1)
                    exp_scores(n, 3)
                    P_hi(n, 2)
                    P_hi(n, 3)
                if m is not None:
                    for t in range(T):
                        normalise1(m, t)
                if b is not None:
                    act.wait_ge(negmax_ready, b.count(1, 1))
                    nc.scalar.activation(w_exp[:], w_log[:], ACT.Exp, bias=neg_max[:], accum_out=w_sum[:]
                                         ).then_inc(wexp_ready, 1)
                if m is not None:
                    hT_hi(m)
                if b is not None and n is not None:
                    act.wait_ge(soft_ready, b.count(1, 1))
                    for t in range(T):
                        if t % 2 == 0:
                            act.wait_ge(v2_psum, b.count(4, t + 2))
                        v2 = ps[:, BANK_V2 + t // 2, (t % 2) * D:(t % 2 + 1) * D]
                        nc.scalar.activation(sv[:, t], v2, ACT.Copy, scale=soft[:, t:t + 1]).then_inc(sv_ready, 1)
                if n is not None:
                    act.wait_ge(nmr2_ready, n.count(1, 1))
                    for t in range(T):
                        nc.scalar.activation(xn2[:, t], x1[n.parity][:, t], ACT.Identity, bias=nmr2[:, t:t + 1],
                                             scale=rstd2[:, t:t + 1]).then_inc(xn2_ready, 1)
            for t in range(T):
                normalise1(batch(0), t)
            hT_hi(batch(0))
            act.wait_ge(set_done, 1)
            steps(act, step)

        @block.vector
        def _(dve):
            def stats(m, t):
                if t == 0:
                    dve.wait_ge(x_landed[m.parity], m.landed())
                nc.vector.bn_stats(st1[:, t], x_in[m.parity][:, t]).then_inc(stats1, 1)

            def variance(n, st, mom, ve, stats_sem, mom_sem, var_sem):
                dve.wait_ge(stats_sem, n.count(4, 4))
                nc.vector.tensor_tensor(mom[:, 0], st[:, :, 1], st[:, :, 4], ALU.add).then_inc(mom_sem, 1)
                nc.vector.tensor_tensor(mom[:, 1], st[:, :, 1], st[:, :, 4], ALU.subtract).then_inc(mom_sem, 1)
                nc.vector.scalar_tensor_tensor(out=mom[:, 2], in0=st[:, :, 2], scalar=D * LN_EPS, in1=st[:, :, 5],
                                               op0=ALU.add, op1=ALU.add).then_inc(mom_sem, 1)
                dve.wait_ge(mom_sem, n.count(4, 2))
                nc.vector.scalar_tensor_tensor(out=mom[:, 3], in0=mom[:, 1], scalar=0.25, in1=mom[:, 1],
                                               op0=ALU.mult, op1=ALU.mult).then_inc(mom_sem, 1)
                dve.wait_ge(mom_sem, n.count(4, 4))
                nc.vector.scalar_tensor_tensor(out=ve[:], in0=mom[:, 2], scalar=1.0 / D, in1=mom[:, 3],
                                               op0=ALU.mult, op1=ALU.add).then_inc(var_sem, 1)

            def neg_mean_rstd(n, mom, rstd, nmr, rstd_sem, nmr_sem):
                dve.wait_ge(rstd_sem, n.count(1, 1))
                nc.vector.scalar_tensor_tensor(out=nmr[:], in0=mom[:, 0], scalar=-0.5, in1=rstd[:],
                                               op0=ALU.mult, op1=ALU.mult).then_inc(nmr_sem, 1)

            def hT_lo(m):
                for k in range(KD):
                    dve.wait_ge(hTh_ready, m.count(2, k + 1))
                    nc.vector.scalar_tensor_tensor(out=hTl[:, k], in0=ps[:, BANK_TR + k], scalar=0.0,
                                                   in1=f32(hTh[:, k]), op0=ALU.max, op1=ALU.subtract
                                                   ).then_inc(hTl_ready, 1)

            def weigh(n, t):
                dve.wait_ge(exp_ready, n.count(4, t + 1))
                if t == 0:
                    dve.wait_ge(adjT_landed[n.parity], n.landed())
                nc.vector.tensor_tensor(Pm[:, t], E[:, t], adjT_in[n.parity][:, t], ALU.mult).then_inc(p_ready, 1)

            def P_lo(n, t):
                dve.wait_ge(ph_ready, n.count(4, t + 1))
                nc.vector.tensor_tensor(Pl[:, t], Pm[:, t], f32(Ph[:, t]), ALU.subtract).then_inc(pl_ready, 1)

            def residual(n, t):
                dve.wait_ge(pv_psum, n.count(4, t + 1))
                nc.vector.reciprocal(row_inv[:, t:t + 1], ps[:, BANK_PROJ + t % 2, D:D + 1]).then_inc(inv_ready, 1)
                dve.wait_ge(inv_ready, n.count(4, t + 1))
                if t == 0:
                    dve.wait_ge(xbv_ready, n.count(1, 1))
                nc.vector.scalar_tensor_tensor(out=x1[n.parity][:, t], in0=ps[:, BANK_PROJ + t % 2, 0:D],
                                               scalar=row_inv[:, t:t + 1], in1=x_bv[:, t],
                                               op0=ALU.mult, op1=ALU.add).then_inc(x1_ready, 1)

            def stats_x1(n, t):
                dve.wait_ge(x1_ready, n.count(4, t + 1))
                nc.vector.bn_stats(st2[:, t], x1[n.parity][:, t]).then_inc(stats2, 1)

            def row_score(n, b, t):
                dve.wait_ge(t_psum, b.count(4, t + 1))
                if t == 0:
                    dve.wait_ge(adjm_ready, b.count(4, 4))
                bank = (BANK_T_LAST if n is None else BANK_S)[t]
                nc.vector.tensor_tensor_reduce(out=w_junk[:, t], in0=ps[:, bank], in1=adj_in[b.parity][:, t],
                                               scale=1.0, scalar=0.0, op0=ALU.mult, op1=ALU.add,
                                               accum_out=w_raw[:, t:t + 1]).then_inc(w_ready, 1)

            def step(n, b, m):
                if n is not None:
                    for k in range(KD):
                        dve.wait_ge(sTh_ready, n.count(2, k + 1))
                        nc.vector.scalar_tensor_tensor(out=sTl[:, k], in0=ps[:, BANK_PROJ + k], scalar=sbias[:, k:k + 1],
                                                       in1=f32(sTh[:, k]), op0=ALU.add, op1=ALU.subtract
                                                       ).then_inc(sTl_ready, 1)
                if b is not None:
                    for k in range(KD):
                        dve.wait_ge(h2Th_ready, b.count(2, k + 1))
                        nc.vector.scalar_tensor_tensor(out=h2Tl[:, k], in0=ps[:, BANK_TR + k], scalar=0.0,
                                                       in1=f32(h2Th[:, k]), op0=ALU.max, op1=ALU.subtract
                                                       ).then_inc(h2Tl_ready, 1)
                if n is not None:
                    for k in range(2):
                        pair = slice(2 * k, 2 * k + 2)
                        banks = slice(BANK_V + 2 * k, BANK_V + 2 * k + 2)
                        dve.wait_ge(vh_ready, n.count(2, k + 1))
                        nc.vector.tensor_tensor(vl[:, pair, 0:D], ps[:, banks, 0:D], f32(vh[:, pair, 0:D]), ALU.subtract
                                                ).then_inc(vl_ready, 1)
                        nc.vector.tensor_scalar(e_row[:, pair], ps[:, banks, D], bqbk[:], None, ALU.add
                                                ).then_inc(e_ready, 1)
                if b is not None:
                    for k in range(KD):
                        dve.wait_ge(s2Th_ready, b.count(2, k + 1))
                        nc.vector.tensor_tensor(s2Tl[:, k], ps[:, BANK_PROJ + k], f32(s2Th[:, k]), ALU.subtract
                                                ).then_inc(s2Tl_ready, 1)
                if m is not None:
                    stats(m, 0)
                    stats(m, 1)
                if n is not None:
                    weigh(n, 0)
                    if m is not None:
                        stats(m, 2)
                        stats(m, 3)
                    weigh(n, 1)
                    P_lo(n, 0)
                    weigh(n, 2)
                    P_lo(n, 1)
                if m is not None:
                    variance(m, st1, mom1, ve1, stats1, moments1, var1)
                if n is not None:
                    weigh(n, 3)
                    P_lo(n, 2)
                if b is not None:
                    row_score(n, b, 0)
                if n is not None:
                    P_lo(n, 3)
                if b is not None:
                    row_score(n, b, 1)
                if m is not None:
                    neg_mean_rstd(m, mom1, rstd1, nmr1, rstd1_ready, nmr1_ready)
                if b is not None:
                    row_score(n, b, 2)
                    row_score(n, b, 3)
                if b is not None:
                    dve.wait_ge(w_ready, b.count(4, 4))
                    nc.vector.tensor_tensor(w_log[:], w_raw[:], mask_scaled[:, bass.ds(b.number * T, T)],
                                            ALU.mult).then_inc(wlog_ready, 1)
                if n is not None:
                    residual(n, 0)
                    stats_x1(n, 0)
                if b is not None:
                    dve.wait_ge(wlogT_psum, b.count(1, 1))
                    nc.vector.tensor_reduce(max4[:], small[0:T, 0:P], AX_X, ALU.max).then_inc(max4_ready, 1)
                    dve.wait_ge(max4_ready, b.count(1, 1))
                    nc.vector.tensor_scalar(neg_diag[:], ident[0:T, 0:T], max4[:], -1.0, ALU.mult, ALU.mult
                                            ).then_inc(diag_ready, 1)
                if n is not None:
                    residual(n, 1)
                    stats_x1(n, 1)
                if b is not None:
                    dve.wait_ge(max_psum, b.count(1, 1))
                    nc.vector.tensor_reduce(neg_max[:], small[:, MAX_COL:MAX_COL + T], AX_X, ALU.min
                                            ).then_inc(negmax_ready, 1)
                if m is not None:
                    hT_lo(m)
                if n is not None:
                    residual(n, 2)
                    stats_x1(n, 2)
                if b is not None:
                    dve.wait_ge(sum_psum, b.count(1, 1))
                    nc.vector.reciprocal(w_inv[:], small[:, SUM_COL:SUM_COL + 1]).then_inc(winv_ready, 1)
                    dve.wait_ge(winv_ready, b.count(1, 1))
                    nc.vector.tensor_scalar(soft[:], w_exp[:], w_inv[:], None, ALU.mult).then_inc(soft_ready, 1)
                if n is not None:
                    residual(n, 3)
                    stats_x1(n, 3)
                    variance(n, st2, mom2, ve2, stats2, moments2, var2)
                    neg_mean_rstd(n, mom2, rstd2, nmr2, rstd2_ready, nmr2_ready)
                if b is not None and n is None:
                    dve.wait_ge(soft_ready, b.count(1, 1))
                    dve.wait_ge(v2_psum, b.count(4, 4))
                    dve.wait_ge(y_free, b.count(16, 16))
                    for t in range(T):
                        v2 = ps[:, BANK_V2 + t // 2, (t % 2) * D:(t % 2 + 1) * D]
                        nc.vector.scalar_tensor_tensor(out=y[:, t], in0=v2, scalar=soft[:, t:t + 1],
                                                       in1=x1[b.parity][:, t], op0=ALU.mult, op1=ALU.add
                                                       ).then_inc(y_ready, 1)
                if b is None:
                    late_weights()

            chain = [0]

            def link(ins):
                chain[0] += 1
                ins.then_inc(set_chain, 1)
                dve.wait_ge(set_chain, chain[0])

            def late_weights():
                dve.wait_ge(late_landed, LATE_LOADS)
                link(nc.vector.tensor_copy(W1h[:], wv1_sb[:]))
                nc.vector.tensor_tensor(W1l[:], wv1_sb[:], f32(W1h[:]), ALU.subtract)
                dve.wait_ge(m1_psum, 1)
                m1 = ps[:, 5, :].rearrange("p (k d) -> p k d", k=KD)
                link(nc.vector.tensor_copy(M1h[:], m1))
                nc.vector.tensor_tensor(M1l[:], m1, f32(M1h[:]), ALU.subtract).then_inc(m1_ready, 1)
                nc.vector.tensor_scalar(mask_scaled[:], ps[:, 4, 0:B * T], INV_SCALE, None, ALU.mult
                                        ).then_inc(m1_ready, 1)
                dve.wait_ge(m1_ready, 2)

            first = batch(0)
            for t in range(T):
                stats(first, t)
            variance(first, st1, mom1, ve1, stats1, moments1, var1)
            nc.vector.memset(vl[:, :, D:VC].bitcast(F32), 0.0)
            nc.vector.memset(Wvl[:, :, D:VC].bitcast(F32), 0.0)
            nc.vector.memset(Wvh[:, :, D:VC].bitcast(F32), 0.0)
            nc.vector.memset(vh[:, :, D + 1:VC].bitcast(F32), 0.0)
            nc.vector.memset(vh[:, :, D:D + 1].bitcast(F32), 1.0).then_inc(v_ones, 1)
            dve.wait_ge(w0_landed, W0_LOADS)
            nc.vector.tensor_tensor(bqbk_col[:], bk_col[:], wq_bq[:, :, D], ALU.mult).then_inc(bqbk_ready, 1)
            neg_mean_rstd(first, mom1, rstd1, nmr1, rstd1_ready, nmr1_ready)
            dve.wait_ge(wv_landed, WV_LOADS)
            link(nc.vector.tensor_copy(Wvh[:, :, 0:D], wvT_sb[:]))
            nc.vector.tensor_tensor(Wvl[:, :, 0:D], wvT_sb[:], f32(Wvh[:, :, 0:D]), ALU.subtract)
            dve.wait_ge(set_psum, 1)
            link(nc.vector.tensor_copy(M0h[:], ps[:, 2:4, 0:D]))
            nc.vector.tensor_tensor(M0l[:], ps[:, 2:4, 0:D], f32(M0h[:]), ALU.subtract)
            link(nc.vector.tensor_copy(Wvh[:, :, D], ps[:, 2:4, D]))
            nc.vector.tensor_tensor(Wvl[:, :, D], ps[:, 2:4, D], f32(Wvh[:, :, D]), ALU.subtract)
            nc.vector.tensor_copy(sbias[:], ps[:, 4, 0:KD])
            nc.vector.tensor_copy(bqbk[:], ps[:, 4, KD:KD + 1]).then_inc(set_done, 1)
            hT_lo(first)
            steps(dve, step)

        @block.tensor
        def _(pe):
            def product(out_ap, pairs, done=None):
                last = 3 * len(pairs) - 1
                i = 0
                for (ah, al), (bh, bl) in pairs:
                    for a, b_ in ((ah, bh), (ah, bl), (al, bh)):
                        mm = nc.tensor.matmul(out_ap, a, b_, start=(i == 0), stop=(i == last))
                        i += 1
                if done is not None:
                    mm.then_inc(done, 1)

            def transposed_rows(src, done):
                for k in range(KD):
                    for t in range(T):
                        mm = nc.tensor.transpose(ps[:, BANK_TR + k, t * P:(t + 1) * P],
                                                 src[:, t, k * P:(k + 1) * P], ident[:])
                    mm.then_inc(done, 1)

            def TX(m):
                pe.wait_ge(xn_ready, m.count(4, 4))
                transposed_rows(xn, hT_psum)

            def project(wh, wl, inh, inl, done):
                for k in range(KD):
                    product(ps[:, BANK_PROJ + k],
                            [((wh[:, q, k * P:(k + 1) * P], wl[:, q, k * P:(k + 1) * P]), (inh[:, q], inl[:, q]))
                             for q in range(KD)], done)

            def scores(ah, al, bh, bl, t, bank, done):
                product(ps[:, bank],
                        [((ah[:, q, t * P:(t + 1) * P], al[:, q, t * P:(t + 1) * P]), (bh[:, q], bl[:, q]))
                         for q in range(KD)], done)

            def S(n, t):
                if t == 0:
                    pe.wait_ge(sTl_ready, n.count(2, 2))
                if t % 2 == 0:
                    pe.wait_ge(e_ready, n.count(2, t // 2 + 1))
                scores(sTh, sTl, hTh, hTl, t, BANK_S[t], s_psum)

            def S2(n, b, t):
                if t == 0:
                    pe.wait_ge(s2Tl_ready, b.count(2, 2))
                if n is not None:
                    pe.wait_ge(exp_ready, n.count(4, t + 1))
                    scores(h2Th, h2Tl, s2Th, s2Tl, t, BANK_S[t], t_psum)
                else:
                    if t >= 2:
                        pe.wait_ge(w_ready, b.count(4, t - 1))
                    scores(h2Th, h2Tl, s2Th, s2Tl, t, BANK_T_LAST[t], t_psum)

            def PV(n, t):
                if t == 0:
                    pe.wait_ge(v_ones, 1)
                    pe.wait_ge(vl_ready, n.count(2, 2))
                    pe.wait_ge(pl_ready, n.count(4, 4))
                if t >= 2:
                    pe.wait_ge(x1_ready, n.count(4, t - 1))
                rows = slice(t * P, (t + 1) * P)
                product(ps[:, BANK_PROJ + t % 2, 0:VC],
                        [((Ph[:, j, rows], Pl[:, j, rows]), (vh[:, j], vl[:, j])) for j in range(T)], pv_psum)

            def V2(b, t):
                rows = slice(t * P, (t + 1) * P)
                product(ps[:, BANK_V2 + t // 2, (t % 2) * D:(t % 2 + 1) * D],
                        [((h2Th[:, q, rows], h2Tl[:, q, rows]), (W1h[:, q], W1l[:, q])) for q in range(KD)], v2_psum)

            def w_transposed(b):
                pe.wait_ge(wlog_ready, b.count(1, 1))
                nc.tensor.matmul(small[0:T, 0:P], w_log[:], ident[:], start=True, stop=True).then_inc(wlogT_psum, 1)

            def maxima(b):
                pe.wait_ge(diag_ready, b.count(1, 1))
                nc.tensor.matmul(small[:, MAX_COL:MAX_COL + T], ones[0:T, :], neg_diag[:], start=True, stop=True
                                 ).then_inc(max_psum, 1)

            def exp_sum(b):
                pe.wait_ge(wexp_ready, b.count(1, 1))
                nc.tensor.matmul(small[:, SUM_COL:SUM_COL + 1], ones[:], w_sum[:], start=True, stop=True
                                 ).then_inc(sum_psum, 1)

            def step(n, b, m):
                if n is not None:
                    pe.wait_ge(hTl_ready, n.count(2, 2))
                    if b is not None:
                        pe.wait_ge(x1_ready, b.count(4, 4))
                    project(M0h, M0l, hTh, hTl, sT_psum)
                if b is not None:
                    pe.wait_ge(m1_ready, 2)
                    pe.wait_ge(xn2_ready, b.count(4, 4))
                    transposed_rows(xn2, h2T_psum)
                if n is not None:
                    pe.wait_ge(sTh_ready, n.count(2, 1))
                    for t in range(T):
                        product(ps[:, BANK_V + t, 0:VC],
                                [((hTh[:, q, t * P:(t + 1) * P], hTl[:, q, t * P:(t + 1) * P]), (Wvh[:, q], Wvl[:, q]))
                                 for q in range(KD)], v_psum)
                if b is not None:
                    pe.wait_ge(h2Tl_ready, b.count(2, 2))
                    if n is not None:
                        pe.wait_ge(sTl_ready, n.count(2, 2))
                    project(M1h, M1l, h2Th, h2Tl, s2T_psum)
                if b is not None and n is None:
                    pe.wait_ge(sv_ready, b.count(4, 0))
                    for t in range(T):
                        V2(b, t)
                if n is not None:
                    for t in range(T):
                        S(n, t)
                if b is None:
                    layer1_weights()
                if b is not None:
                    for t in range(T):
                        S2(n, b, t)
                if n is not None:
                    PV(n, 0)
                if b is not None:
                    w_transposed(b)
                if n is not None:
                    PV(n, 1)
                if b is not None:
                    maxima(b)
                if m is not None:
                    TX(m)
                if n is not None:
                    PV(n, 2)
                if b is not None:
                    exp_sum(b)
                if n is not None:
                    PV(n, 3)
                    if b is not None:
                        for t in range(T):
                            V2(b, t)

            def layer1_weights():
                pe.wait_ge(late_landed, LATE_LOADS)
                pe.wait_ge(exp_ready, 2)
                for k in range(KD):
                    for q in range(KD):
                        nc.tensor.matmul(ps[:, 5, k * D:(k + 1) * D], wqkT_sb[:, KD + q, k * P:(k + 1) * P],
                                         wqkT_sb[:, q], start=(q == 0), stop=(q == KD - 1))
                nc.tensor.transpose(ps[:, 4, 0:B * T], mask_rows[:], ident[0:B * T, 0:B * T]).then_inc(m1_psum, 1)

            pe.wait_ge(const_ready, 4)
            pe.wait_ge(w0_landed, W0_LOADS)
            for k in range(KD):
                for q in range(KD):
                    nc.tensor.matmul(ps[:, 2 + k, 0:D + 1], wk_sb[:, q, k * P:(k + 1) * P], wq_bq[:, q],
                                     start=(q == 0), stop=(q == KD - 1))
            TX(batch(0))
            for k in range(KD):
                for q in range(KD):
                    nc.tensor.matmul(ps[:, 4, k:k + 1], wq_bq[:, q, k * P:(k + 1) * P], bk_col[:, q:q + 1],
                                     start=(q == 0), stop=(q == KD - 1))
            pe.wait_ge(bqbk_ready, 1)
            for q in range(KD):
                mm = nc.tensor.matmul(ps[:, 4, KD:KD + 1], ones[:], bqbk_col[:, q:q + 1],
                                      start=(q == 0), stop=(q == KD - 1))
            mm.then_inc(set_psum, 1)
            pe.wait_ge(set_done, 1)
            steps(pe, step)


def kernel(x, adj, nodemask, L0_gnn_Wq_w, L0_gnn_Wq_b, L0_gnn_Wk_w, L0_gnn_Wk_b, L0_gnn_Wv_w, L0_gnn_Wv_b,
           L1_gnn_Wqk, L1_gnn_Wv):
    import numpy as np
    import concourse.bacc as bacc
    from concourse.bass_utils import run_bass_kernel_spmd

    arrays = {
        "x": x, "adj": adj, "adjT": np.transpose(adj, (0, 2, 1)), "nodemask": nodemask,
        "wq": L0_gnn_Wq_w, "bq": L0_gnn_Wq_b, "wk": L0_gnn_Wk_w, "bk": L0_gnn_Wk_b,
        "wvT": np.transpose(L0_gnn_Wv_w), "bv": L0_gnn_Wv_b,
        "wqkT": np.transpose(L1_gnn_Wqk), "wv1": L1_gnn_Wv,
    }
    arrays = {name: np.ascontiguousarray(a) for name, a in arrays.items()}
    nc = bacc.Bacc("TRN2", target_bir_lowering=False, num_devices=1)
    ins = [nc.dram_tensor(name, a.shape, F32, kind="ExternalInput").ap() for name, a in arrays.items()]
    out = nc.dram_tensor("out", x.shape, F32, kind="ExternalOutput").ap()
    graph_layers_kernel(nc, *ins, out)
    result = run_bass_kernel_spmd(nc, [arrays], core_ids=[0])
    return result.results[0]["out"]
```

```python
from contextlib import ExitStack

import concourse.bass as bass
from concourse import mybir

F32 = mybir.dt.float32
F32R = mybir.dt.float32r
ALU = mybir.AluOpType
ACT = mybir.ActivationFunctionType
AX_X = mybir.AxisListType.X

P = 128
LN_EPS = 1e-5


class Batch:

    def __init__(self, number, half, parity):
        self.number, self.half, self.parity = number, half, parity

    def count(self, per_batch, k):
        return self.number * per_batch + k

    def landed(self):
        return (self.half + 1) * 16


def batch(n):
    return Batch(n, n // 2, n % 2)


def graph_layers_kernel(nc, x, adj, adjT, nodemask, wq, bq, wk, bk, wvT, bv, wqkT, wv1, out):
    B, N, D = x.shape
    T = N // P
    KD = D // P
    VC = D + 2
    INV_SCALE = 1.0 / float(D) ** 0.5
    assert T == 4 and KD == 2 and N == 512 and D == 256 and B % 2 == 0 and B >= 4

    x_rows = x.rearrange("b (t p) d -> b p t d", p=P)
    adj_rows = adj.rearrange("b (t p) j -> b p t j", p=P)
    adjT_rows = adjT.rearrange("b (t p) i -> b p t i", p=P)
    out_rows = out.rearrange("b (t p) d -> b p t d", p=P)

    with ExitStack() as ctx:
        def sb(name, shape, dt=F32):
            return ctx.enter_context(nc.sbuf_tensor(name, shape, dt))

        def sem(name):
            return ctx.enter_context(nc.semaphore(name))

        ps = ctx.enter_context(nc.psum_tensor("ps", [P, 8, 512], F32))
        BANK_TR = 0
        BANK_PROJ = 2
        BANK_V = 4
        BANK_S = (4, 5, 6, 7)
        BANK_S2_LAST = (7, 2, 3, 6)
        BANK_V2 = 4
        BANK_V2_LAST = 0
        small = ps[:, 6, :]
        MAX_COL, SUM_COL = P, P + 8

        ident = sb("ident", [P, P])
        ones = sb("ones", [P, P])
        neg_half = sb("neg_half", [P, T])
        wk_sb = sb("wk_sb", [P, KD, D])
        wq_bq = sb("wq_bq", [P, KD, D + 1])
        bk_col = sb("bk_col", [P, KD])
        bqbk_col = sb("bqbk_col", [P, KD])
        wvT_sb = sb("wvT_sb", [P, KD, D])
        wqkT_sb = sb("wqkT_sb", [P, 2 * KD, D])
        wv1_sb = sb("wv1_sb", [P, KD, D])
        mask_rows = sb("mask_rows", [B * T, P])
        mask_scaled = sb("mask_scaled", [P, B * T])
        bv_all = sb("bv_all", [P, D])
        M0h, M0l = sb("M0h", [P, KD, D], F32R), sb("M0l", [P, KD, D], F32R)
        M1h, M1l = sb("M1h", [P, KD, D], F32R), sb("M1l", [P, KD, D], F32R)
        Wvh, Wvl = sb("Wvh", [P, KD, VC], F32R), sb("Wvl", [P, KD, VC], F32R)
        W1h, W1l = sb("W1h", [P, KD, D], F32R), sb("W1l", [P, KD, D], F32R)
        sbias = sb("sbias", [P, KD])
        bqbk = sb("bqbk", [P, 1])

        x_in = [sb(f"x_in{i}", [P, T, D]) for i in range(2)]
        adjT_in = [sb(f"adjT_in{i}", [P, T, N]) for i in range(2)]
        adj_in = [sb(f"adj_in{i}", [P, T, N]) for i in range(2)]
        mask_all = [sb(f"mask_all{i}", [P, N]) for i in range(2)]
        x1 = [sb(f"x1_{i}", [P, T, D]) for i in range(2)]
        x_bv = sb("x_bv", [P, T, D])
        xn, xn2 = sb("xn", [P, T, D]), sb("xn2", [P, T, D])
        hTh, hTl = sb("hTh", [P, KD, N], F32R), sb("hTl", [P, KD, N], F32R)
        h2Th, h2Tl = sb("h2Th", [P, KD, N], F32R), sb("h2Tl", [P, KD, N], F32R)
        sTh, sTl = sb("sTh", [P, KD, N], F32R), sb("sTl", [P, KD, N], F32R)
        s2Th, s2Tl = sb("s2Th", [P, KD, N], F32R), sb("s2Tl", [P, KD, N], F32R)
        vh, vl = sb("vh", [P, T, VC], F32R), sb("vl", [P, T, VC], F32R)
        e_row = sb("e_row", [P, T])
        E = sb("E", [P, T, N])
        Pm = sb("Pm", [P, T, N])
        Ph, Pl = sb("Ph", [P, T, N], F32R), sb("Pl", [P, T, N], F32R)
        row_inv = sb("row_inv", [P, T])
        st1, st2 = sb("st1", [P, T, 6]), sb("st2", [P, T, 6])
        mom1, mom2 = sb("mom1", [P, 4, T]), sb("mom2", [P, 4, T])
        ve1, ve2 = sb("ve1", [P, T]), sb("ve2", [P, T])
        rstd1, rstd2 = sb("rstd1", [P, T]), sb("rstd2", [P, T])
        nmr1, nmr2 = sb("nmr1", [P, T]), sb("nmr2", [P, T])
        w_products = sb("w_products", [P, T, N])
        w_raw, w_log = sb("w_raw", [P, T]), sb("w_log", [P, T])
        max4, neg_max4 = sb("max4", [T, 1]), sb("neg_max4", [T, P])
        neg_max = sb("neg_max", [P, 1])
        w_exp, w_sum, w_inv, soft = sb("w_exp", [P, T]), sb("w_sum", [P, 1]), sb("w_inv", [P, 1]), sb("soft", [P, T])
        sv = sb("sv", [P, T, D])
        y = sb("y", [P, T, D])

        w0_landed, wv_landed, late_landed = sem("w0_landed"), sem("wv_landed"), sem("late_landed")
        const_ready, v_ones = sem("const_ready"), sem("v_ones")
        bqbk_ready, weight_hi = sem("bqbk_ready"), sem("weight_hi")
        m1_psum, m1h_ready, m1_ready = sem("m1_psum"), sem("m1h_ready"), sem("m1_ready")
        scaled_mask_ready = sem("scaled_mask_ready")
        m0_psum, m0h_ready, m0_ready = sem("m0_psum"), sem("m0h_ready"), sem("m0_ready")
        bias_psum, bias_ready = sem("bias_psum"), sem("bias_ready")
        x_landed = [sem(f"x_landed{i}") for i in range(2)]
        adjT_landed = [sem(f"adjT_landed{i}") for i in range(2)]
        adj_landed = [sem(f"adj_landed{i}") for i in range(2)]
        mask_landed = [sem(f"mask_landed{i}") for i in range(2)]
        stats1, moments1, stats2, moments2 = sem("stats1"), sem("moments1"), sem("stats2"), sem("moments2")
        var1, rstd1_ready, nmr1_ready = sem("var1"), sem("rstd1_ready"), sem("nmr1_ready")
        var2, rstd2_ready, nmr2_ready = sem("var2"), sem("rstd2_ready"), sem("nmr2_ready")
        xn_ready, xn2_ready = sem("xn_ready"), sem("xn2_ready")
        hT_psum, hTh_ready, hTl_ready = sem("hT_psum"), sem("hTh_ready"), sem("hTl_ready")
        h2T_psum, h2Th_ready, h2Tl_ready = sem("h2T_psum"), sem("h2Th_ready"), sem("h2Tl_ready")
        sT_psum, sTh_ready, sTl_ready = sem("sT_psum"), sem("sTh_ready"), sem("sTl_ready")
        s2T_psum, s2Th_ready, s2Tl_ready = sem("s2T_psum"), sem("s2Th_ready"), sem("s2Tl_ready")
        v_psum = sem("v_psum")
        vh_ready, vl_ready, e_ready = sem("vh_ready"), sem("vl_ready"), sem("e_ready")
        s_psum, exp_ready, p_ready = sem("s_psum"), sem("exp_ready"), sem("p_ready")
        ph_ready, pl_ready = sem("ph_ready"), sem("pl_ready")
        pv_psum, inv_ready, x1_ready = sem("pv_psum"), sem("inv_ready"), sem("x1_ready")
        xbv_ready, adjm_ready = sem("xbv_ready"), sem("adjm_ready")
        s2_psum, w_ready = sem("s2_psum"), sem("w_ready")
        wlog_ready, wlogT_psum = sem("wlog_ready"), sem("wlogT_psum")
        max4_ready, negmax4_ready = sem("max4_ready"), sem("negmax4_ready")
        max_psum, negmax_ready, wexp_ready = sem("max_psum"), sem("negmax_ready"), sem("wexp_ready")
        sum_psum, winv_ready, soft_ready = sem("sum_psum"), sem("winv_ready"), sem("soft_ready")
        v2_psum, y_ready = sem("v2_psum"), sem("y_ready")
        sv_ready = sem("sv_ready")
        y_free = sem("y_free")

        def f32(t):
            return t.bitcast(F32)

        def v2_rows(t, first_bank=BANK_V2):
            return ps[:, first_bank + t // 2, (t % 2) * D:(t % 2 + 1) * D]

        def xn2_on_act(b):
            return 0 if b is None else T // 2

        m1_rows = ps[:, 5, :].rearrange("p (k d) -> p k d", k=KD)

        def steps(eng, step, finish=None):
            step(batch(0), None, batch(1))
            with eng.Fori(0, (B - 2) // 2) as g:
                step(Batch(g * 2 + 1, g, 1), Batch(g * 2, g, 0), Batch(g * 2 + 2, g + 1, 0))
                step(Batch(g * 2 + 2, g + 1, 0), Batch(g * 2 + 1, g, 1), Batch(g * 2 + 3, g + 1, 1))
            step(batch(B - 1), batch(B - 2), None)
            if finish is not None:
                finish(batch(B - 2), batch(B - 1))

        W0_LOADS, WV_LOADS, LATE_LOADS = 4 * 16, 16, 4 * 16
        block = ctx.enter_context(nc.Block())

        @block.sync
        def _(sp):
            def load_x(m):
                sp.dma_start(x_in[m.parity][:], x_rows[m.number]).then_inc(x_landed[m.parity], 16)

            def load_adjT(m):
                sp.dma_start(adjT_in[m.parity][:], adjT_rows[m.number]).then_inc(adjT_landed[m.parity], 16)

            def load_adj(m):
                sp.dma_start(mask_all[m.parity][:], nodemask[bass.ds(m.number, 1), :].to_broadcast([P, N])
                             ).then_inc(mask_landed[m.parity], 16)
                sp.dma_start(adj_in[m.parity][:], adj_rows[m.number]).then_inc(adj_landed[m.parity], 16)

            def step(n, b, m):
                if b is None:
                    load_adjT(m)
                    load_adj(m)
                elif m is not None:
                    sp.wait_ge(x1_ready, b.count(4, 4))
                    load_x(m)
                    load_adjT(m)
                    sp.wait_ge(w_ready, b.count(4, 4))
                    load_adj(m)
                if b is not None:
                    sp.wait_ge(y_ready, b.count(4, 4))
                    sp.dma_start(out_rows[b.number], y[:]).then_inc(y_free, 16)

            def finish(b, last):
                for t in range(T):
                    sp.wait_ge(y_ready, last.count(4, t + 1))
                    sp.dma_start(out_rows[last.number, :, t], y[:, t]).then_inc(y_free, 16)

            def load_weights(*pairs, landed, **how):
                for dst, src in pairs:
                    sp.dma_start(dst, src, **how).then_inc(landed, 16)

            load_x(batch(0))
            load_weights((wk_sb[:], wk.rearrange("(k p) d -> p k d", p=P)),
                         (wq_bq[:, :, 0:D], wq.rearrange("(k p) d -> p k d", p=P)), landed=w0_landed)
            load_weights((wq_bq[:, :, D:D + 1], bq.rearrange("(k p a) -> p k a", p=P, a=1)),
                         (bk_col[:].rearrange("p (k a) -> p k a", a=1), bk.rearrange("(k p a) -> p k a", p=P, a=1)),
                         landed=w0_landed, allow_slow_non_contiguous=True)
            load_weights((wvT_sb[:], wvT.rearrange("(k p) d -> p k d", p=P)), landed=wv_landed)
            load_adjT(batch(0))
            load_x(batch(1))
            load_weights((bv_all[:], bv.rearrange("(a d) -> a d", a=1).to_broadcast([P, D])),
                         (mask_rows[:], nodemask.rearrange("b (t p) -> (b t) p", p=P)),
                         (wqkT_sb[:], wqkT.rearrange("(k p) d -> p k d", p=P)),
                         (wv1_sb[:], wv1.rearrange("(k p) d -> p k d", p=P)), landed=late_landed)
            load_adj(batch(0))
            steps(sp, step, finish)
            sp.wait_ge(y_free, 16 * (B + T))

        @block.gpsimd
        def _(pool):
            nc.gpsimd.memset(ident[:], 0.0).then_inc(const_ready, 1)
            nc.gpsimd.memset(ones[:], 1.0).then_inc(const_ready, 1)
            nc.gpsimd.memset(neg_half[:], -0.5).then_inc(const_ready, 1)
            pool.wait_ge(const_ready, 3)
            nc.gpsimd.affine_select(out=ident[:], in_=ident[:], compare_op=ALU.not_equal, fill=1.0, base=0,
                                    pattern=[[-1, P]], channel_multiplier=1).then_inc(const_ready, 1)
            pool.sem_inc(y_free, 16)
            pool.sem_inc(sv_ready, 4)

            def power1(m):
                pool.wait_ge(var1, m.count(1, 1))
                nc.gpsimd.tensor_tensor(rstd1[:], ve1[:], neg_half[:], ALU.pow).then_inc(rstd1_ready, 1)

            def adj_mask(n, t):
                adj_t = adj_in[n.parity][:, t]
                nc.gpsimd.tensor_tensor(adj_t, adj_t, mask_all[n.parity][:], ALU.mult).then_inc(adjm_ready, 1)

            def step(n, b, m):
                if b is None:
                    power1(m)
                    pool.wait_ge(late_landed, LATE_LOADS)
                else:
                    pool.wait_ge(x1_ready, b.count(4, 4))
                pool.wait_ge(x_landed[n.parity], n.landed())
                nc.gpsimd.tensor_tensor(x_bv[:], x_in[n.parity][:],
                                        bv_all[:].rearrange("p (o d) -> p o d", o=1).to_broadcast([P, T, D]),
                                        ALU.add).then_inc(xbv_ready, 1)
                pool.wait_ge(adj_landed[n.parity], n.landed())
                pool.wait_ge(mask_landed[n.parity], n.landed())
                for t in range(T):
                    adj_mask(n, t)
                if b is not None and m is not None:
                    power1(m)
                pool.wait_ge(var2, n.count(1, 1))
                nc.gpsimd.tensor_tensor(rstd2[:], ve2[:], neg_half[:], ALU.pow).then_inc(rstd2_ready, 1)
                if b is not None:
                    pool.wait_ge(y_free, b.count(16, 16))
                    for t in range(T):
                        pool.wait_ge(sv_ready, b.count(4, 4 + t + 1))
                        nc.gpsimd.tensor_tensor(y[:, t], sv[:, t], x1[b.parity][:, t], ALU.add).then_inc(y_ready, 1)

            power1(batch(0))
            steps(pool, step)

        @block.scalar
        def _(act):
            def normalise1(m, t):
                if t == 0:
                    act.wait_ge(nmr1_ready, m.count(1, 1))
                nc.scalar.activation(xn[:, t], x_in[m.parity][:, t], ACT.Identity, bias=nmr1[:, t:t + 1],
                                     scale=rstd1[:, t:t + 1]).then_inc(xn_ready, 1)

            def hT_hi(m):
                for k in range(KD):
                    act.wait_ge(hT_psum, m.count(2, k + 1))
                    nc.scalar.activation(hTh[:, k], ps[:, BANK_TR + k], ACT.Relu).then_inc(hTh_ready, 1)

            def exp_scores(n, t):
                act.wait_ge(s_psum, n.count(4, t + 1))
                act.wait_ge(e_ready, n.count(2, t // 2 + 1))
                nc.scalar.activation(E[:, t], ps[:, BANK_S[t]], ACT.Exp, bias=e_row[:, t:t + 1]
                                     ).then_inc(exp_ready, 1)

            def P_hi(n, t):
                act.wait_ge(p_ready, n.count(4, t + 1))
                nc.scalar.activation(Ph[:, t], Pm[:, t], ACT.Identity).then_inc(ph_ready, 1)

            def h2T_hi(b, h2h=h2Th):
                for k in range(KD):
                    act.wait_ge(h2T_psum, b.count(2, k + 1))
                    nc.scalar.activation(h2h[:, k], ps[:, BANK_TR + k], ACT.Relu).then_inc(h2Th_ready, 1)

            def s2T_hi(b):
                for k in range(KD):
                    act.wait_ge(s2T_psum, b.count(2, k + 1))
                    nc.scalar.activation(s2Th[:, k], ps[:, BANK_PROJ + k], ACT.Identity).then_inc(s2Th_ready, 1)

            def exp_w(b):
                act.wait_ge(negmax_ready, b.count(1, 1))
                nc.scalar.activation(w_exp[:], w_log[:], ACT.Exp, bias=neg_max[:], accum_out=w_sum[:]
                                     ).then_inc(wexp_ready, 1)

            def softmax_v(b):
                act.wait_ge(soft_ready, b.count(1, 1))
                for t in range(T):
                    if t % 2 == 0:
                        act.wait_ge(v2_psum, b.count(4, t + 2))
                    nc.scalar.activation(sv[:, t], v2_rows(t), ACT.Copy, scale=soft[:, t:t + 1]).then_inc(sv_ready, 1)

            def step(n, b, m):
                for k in range(KD):
                    act.wait_ge(sT_psum, n.count(2, k + 1))
                    nc.scalar.activation(sTh[:, k], ps[:, BANK_PROJ + k], ACT.Identity, bias=sbias[:, k:k + 1]
                                         ).then_inc(sTh_ready, 1)
                for k in range(2):
                    act.wait_ge(v_psum, n.count(4, 2 * k + 2))
                    nc.scalar.activation(vh[:, 2 * k:2 * k + 2, 0:D], ps[:, BANK_V + 2 * k:BANK_V + 2 * k + 2, 0:D],
                                         ACT.Identity).then_inc(vh_ready, 1)
                if b is None:
                    for t in range(T):
                        normalise1(m, t)
                else:
                    h2T_hi(b)
                exp_scores(n, 0)
                exp_scores(n, 1)
                P_hi(n, 0)
                P_hi(n, 1)
                if b is not None:
                    s2T_hi(b)
                exp_scores(n, 2)
                exp_scores(n, 3)
                P_hi(n, 2)
                P_hi(n, 3)
                if b is not None and m is not None:
                    for t in range(T):
                        normalise1(m, t)
                if m is not None:
                    hT_hi(m)
                if b is None:
                    act.wait_ge(m1_psum, 1)
                    nc.scalar.activation(M1h[:], m1_rows, ACT.Identity).then_inc(m1h_ready, 1)
                    nc.scalar.activation(mask_scaled[:], ps[:, 4, 0:B * T], ACT.Copy, scale=INV_SCALE
                                         ).then_inc(scaled_mask_ready, 1)
                if b is not None and m is not None:
                    exp_w(b)
                    softmax_v(b)
                if b is not None:
                    act.wait_ge(nmr2_ready, n.count(1, 1))
                for t in range(xn2_on_act(b)):
                    nc.scalar.activation(xn2[:, t], x1[n.parity][:, t], ACT.Identity, bias=nmr2[:, t:t + 1],
                                         scale=rstd2[:, t:t + 1]).then_inc(xn2_ready, 1)

            def finish(b, last):
                h2T_hi(last, hTh)
                s2T_hi(last)
                exp_w(b)
                softmax_v(b)
                exp_w(last)

            normalise1(batch(0), 0)
            normalise1(batch(0), 1)
            act.wait_ge(m0_psum, 1)
            nc.scalar.activation(M0h[:], ps[:, 2:4, 0:D], ACT.Identity).then_inc(m0h_ready, 1)
            hT_hi(batch(0))
            act.wait_ge(bias_ready, 1)
            steps(act, step, finish)

        @block.vector
        def _(dve):
            def stats(m, t):
                if t == 0:
                    dve.wait_ge(x_landed[m.parity], m.landed())
                nc.vector.bn_stats(st1[:, t], x_in[m.parity][:, t]).then_inc(stats1, 1)

            def variance(n, st, mom, ve, stats_sem, mom_sem, var_sem):
                dve.wait_ge(stats_sem, n.count(4, 4))
                nc.vector.tensor_tensor(mom[:, 0], st[:, :, 1], st[:, :, 4], ALU.add).then_inc(mom_sem, 1)
                nc.vector.tensor_tensor(mom[:, 1], st[:, :, 1], st[:, :, 4], ALU.subtract).then_inc(mom_sem, 1)
                nc.vector.scalar_tensor_tensor(out=mom[:, 2], in0=st[:, :, 2], scalar=D * LN_EPS, in1=st[:, :, 5],
                                               op0=ALU.add, op1=ALU.add).then_inc(mom_sem, 1)
                dve.wait_ge(mom_sem, n.count(4, 2))
                nc.vector.scalar_tensor_tensor(out=mom[:, 3], in0=mom[:, 1], scalar=0.25, in1=mom[:, 1],
                                               op0=ALU.mult, op1=ALU.mult).then_inc(mom_sem, 1)
                dve.wait_ge(mom_sem, n.count(4, 4))
                nc.vector.scalar_tensor_tensor(out=ve[:], in0=mom[:, 2], scalar=1.0 / D, in1=mom[:, 3],
                                               op0=ALU.mult, op1=ALU.add).then_inc(var_sem, 1)

            def neg_mean_rstd(n, mom, rstd, nmr, rstd_sem, nmr_sem):
                dve.wait_ge(rstd_sem, n.count(1, 1))
                nc.vector.scalar_tensor_tensor(out=nmr[:], in0=mom[:, 0], scalar=-0.5, in1=rstd[:],
                                               op0=ALU.mult, op1=ALU.mult).then_inc(nmr_sem, 1)

            def hT_lo(m, k):
                dve.wait_ge(hTh_ready, m.count(2, k + 1))
                nc.vector.scalar_tensor_tensor(out=hTl[:, k], in0=ps[:, BANK_TR + k], scalar=0.0,
                                               in1=f32(hTh[:, k]), op0=ALU.max, op1=ALU.subtract
                                               ).then_inc(hTl_ready, 1)

            def weigh(n, t):
                dve.wait_ge(exp_ready, n.count(4, t + 1))
                if t == 0:
                    dve.wait_ge(adjT_landed[n.parity], n.landed())
                nc.vector.tensor_tensor(Pm[:, t], E[:, t], adjT_in[n.parity][:, t], ALU.mult).then_inc(p_ready, 1)

            def P_lo(n, t):
                dve.wait_ge(ph_ready, n.count(4, t + 1))
                nc.vector.tensor_tensor(Pl[:, t], Pm[:, t], f32(Ph[:, t]), ALU.subtract).then_inc(pl_ready, 1)

            def residual(n, t):
                dve.wait_ge(pv_psum, n.count(4, t + 1))
                nc.vector.reciprocal(row_inv[:, t:t + 1], ps[:, BANK_PROJ + t % 2, D:D + 1]).then_inc(inv_ready, 1)
                dve.wait_ge(inv_ready, n.count(4, t + 1))
                if t == 0:
                    dve.wait_ge(xbv_ready, n.count(1, 1))
                nc.vector.scalar_tensor_tensor(out=x1[n.parity][:, t], in0=ps[:, BANK_PROJ + t % 2, 0:D],
                                               scalar=row_inv[:, t:t + 1], in1=x_bv[:, t],
                                               op0=ALU.mult, op1=ALU.add).then_inc(x1_ready, 1)

            def stats_x1(n, t):
                dve.wait_ge(x1_ready, n.count(4, t + 1))
                nc.vector.bn_stats(st2[:, t], x1[n.parity][:, t]).then_inc(stats2, 1)

            def row_score(n, b, t):
                dve.wait_ge(s2_psum, b.count(4, t + 1))
                if t == 0:
                    dve.wait_ge(adjm_ready, b.count(4, 4))
                bank = (BANK_S2_LAST if n is None else BANK_S)[t]
                nc.vector.tensor_tensor_reduce(out=w_products[:, t], in0=ps[:, bank], in1=adj_in[b.parity][:, t],
                                               scale=1.0, scalar=0.0, op0=ALU.mult, op1=ALU.add,
                                               accum_out=w_raw[:, t:t + 1]).then_inc(w_ready, 1)

            def h2T_lo(b, h2h=h2Th, h2l=h2Tl):
                for k in range(KD):
                    dve.wait_ge(h2Th_ready, b.count(2, k + 1))
                    nc.vector.scalar_tensor_tensor(out=h2l[:, k], in0=ps[:, BANK_TR + k], scalar=0.0,
                                                   in1=f32(h2h[:, k]), op0=ALU.max, op1=ALU.subtract
                                                   ).then_inc(h2Tl_ready, 1)

            def s2T_lo(b):
                for k in range(KD):
                    dve.wait_ge(s2Th_ready, b.count(2, k + 1))
                    nc.vector.tensor_tensor(s2Tl[:, k], ps[:, BANK_PROJ + k], f32(s2Th[:, k]), ALU.subtract
                                            ).then_inc(s2Tl_ready, 1)

            def scaled_scores(b):
                dve.wait_ge(scaled_mask_ready, 1)
                dve.wait_ge(w_ready, b.count(4, 4))
                nc.vector.tensor_tensor(w_log[:], w_raw[:], mask_scaled[:, bass.ds(b.number * T, T)],
                                        ALU.mult).then_inc(wlog_ready, 1)

            def tile_maxima(b):
                dve.wait_ge(wlogT_psum, b.count(1, 1))
                nc.vector.tensor_reduce(max4[:], small[0:T, 0:P], AX_X, ALU.max).then_inc(max4_ready, 1)
                dve.wait_ge(max4_ready, b.count(1, 1))
                nc.vector.tensor_scalar(neg_max4[:], ones[0:T, :], max4[:], -1.0, ALU.mult, ALU.mult
                                        ).then_inc(negmax4_ready, 1)

            def maximum(b):
                dve.wait_ge(max_psum, b.count(1, 1))
                nc.vector.tensor_reduce(neg_max[:], small[:, MAX_COL:MAX_COL + T], AX_X, ALU.min
                                        ).then_inc(negmax_ready, 1)

            def softmax(b):
                dve.wait_ge(sum_psum, b.count(1, 1))
                nc.vector.reciprocal(w_inv[:], small[:, SUM_COL:SUM_COL + 1]).then_inc(winv_ready, 1)
                dve.wait_ge(winv_ready, b.count(1, 1))
                nc.vector.tensor_scalar(soft[:], w_exp[:], w_inv[:], None, ALU.mult).then_inc(soft_ready, 1)

            def normalise2(n, b):
                dve.wait_ge(nmr2_ready, n.count(1, 1))
                for t in range(xn2_on_act(b), T):
                    nc.vector.tensor_scalar(xn2[:, t], x1[n.parity][:, t], rstd2[:, t:t + 1], nmr2[:, t:t + 1],
                                            ALU.mult, ALU.add).then_inc(xn2_ready, 1)

            def step(n, b, m):
                if b is None:
                    for t in range(T):
                        stats(m, t)
                    variance(m, st1, mom1, ve1, stats1, moments1, var1)
                for k in range(KD):
                    dve.wait_ge(sTh_ready, n.count(2, k + 1))
                    nc.vector.scalar_tensor_tensor(out=sTl[:, k], in0=ps[:, BANK_PROJ + k], scalar=sbias[:, k:k + 1],
                                                   in1=f32(sTh[:, k]), op0=ALU.add, op1=ALU.subtract
                                                   ).then_inc(sTl_ready, 1)
                if b is None:
                    neg_mean_rstd(m, mom1, rstd1, nmr1, rstd1_ready, nmr1_ready)
                for k in range(2):
                    pair = slice(2 * k, 2 * k + 2)
                    banks = slice(BANK_V + 2 * k, BANK_V + 2 * k + 2)
                    dve.wait_ge(vh_ready, n.count(2, k + 1))
                    nc.vector.tensor_tensor(vl[:, pair, 0:D], ps[:, banks, 0:D], f32(vh[:, pair, 0:D]), ALU.subtract
                                            ).then_inc(vl_ready, 1)
                    nc.vector.tensor_scalar(e_row[:, pair], ps[:, banks, D], bqbk[:], None, ALU.add
                                            ).then_inc(e_ready, 1)
                if b is None:
                    split_w1()
                else:
                    h2T_lo(b)
                    if m is not None:
                        stats(m, 0)
                        stats(m, 1)
                weigh(n, 0)
                weigh(n, 1)
                P_lo(n, 0)
                P_lo(n, 1)
                if b is not None:
                    s2T_lo(b)
                    if m is not None:
                        stats(m, 2)
                        stats(m, 3)
                        variance(m, st1, mom1, ve1, stats1, moments1, var1)
                weigh(n, 2)
                weigh(n, 3)
                P_lo(n, 2)
                P_lo(n, 3)
                if b is None:
                    hT_lo(m, 0)
                    hT_lo(m, 1)
                else:
                    row_score(n, b, 0)
                    if m is not None:
                        neg_mean_rstd(m, mom1, rstd1, nmr1, rstd1_ready, nmr1_ready)
                    row_score(n, b, 1)
                    if m is not None:
                        row_score(n, b, 2)
                        row_score(n, b, 3)
                        scaled_scores(b)
                softmax_here = b is not None and m is not None
                residual(n, 0)
                stats_x1(n, 0)
                residual(n, 1)
                if softmax_here:
                    tile_maxima(b)
                stats_x1(n, 1)
                if softmax_here:
                    hT_lo(m, 0)
                    hT_lo(m, 1)
                residual(n, 2)
                stats_x1(n, 2)
                if softmax_here:
                    maximum(b)
                residual(n, 3)
                stats_x1(n, 3)
                variance(n, st2, mom2, ve2, stats2, moments2, var2)
                if softmax_here:
                    softmax(b)
                if b is None:
                    dve.wait_ge(m1h_ready, 1)
                    nc.vector.tensor_tensor(M1l[:], m1_rows, f32(M1h[:]), ALU.subtract).then_inc(m1_ready, 1)
                if b is not None and m is None:
                    row_score(n, b, 2)
                neg_mean_rstd(n, mom2, rstd2, nmr2, rstd2_ready, nmr2_ready)
                normalise2(n, b)
                if b is not None and m is None:
                    row_score(n, b, 3)
                    scaled_scores(b)

            def finish(b, last):
                h2T_lo(last, hTh, hTl)
                tile_maxima(b)
                s2T_lo(last)
                maximum(b)
                softmax(b)
                for t in range(T):
                    row_score(None, last, t)
                scaled_scores(last)
                tile_maxima(last)
                maximum(last)
                softmax(last)
                dve.wait_ge(soft_ready, last.count(1, 1))
                dve.wait_ge(v2_psum, last.count(4, 4))
                dve.wait_ge(y_free, last.count(16, 16))
                for t in range(T):
                    nc.vector.scalar_tensor_tensor(out=y[:, t], in0=v2_rows(t, BANK_V2_LAST), scalar=soft[:, t:t + 1],
                                                   in1=x1[last.parity][:, t], op0=ALU.mult, op1=ALU.add
                                                   ).then_inc(y_ready, 1)

            def split_w1():
                dve.wait_ge(late_landed, LATE_LOADS)
                nc.vector.tensor_copy(W1h[:], wv1_sb[:]).then_inc(weight_hi, 1)
                dve.wait_ge(weight_hi, 3)
                nc.vector.tensor_tensor(W1l[:], wv1_sb[:], f32(W1h[:]), ALU.subtract)

            first = batch(0)
            for t in range(T):
                stats(first, t)
            variance(first, st1, mom1, ve1, stats1, moments1, var1)
            nc.vector.memset(vl[:, :, D:VC].bitcast(F32), 0.0)
            nc.vector.memset(Wvl[:, :, D:VC].bitcast(F32), 0.0)
            nc.vector.memset(Wvh[:, :, D:VC].bitcast(F32), 0.0)
            nc.vector.memset(vh[:, :, D + 1:VC].bitcast(F32), 0.0)
            nc.vector.memset(vh[:, :, D:D + 1].bitcast(F32), 1.0).then_inc(v_ones, 1)
            dve.wait_ge(w0_landed, W0_LOADS)
            nc.vector.tensor_tensor(bqbk_col[:], bk_col[:], wq_bq[:, :, D], ALU.mult).then_inc(bqbk_ready, 1)
            neg_mean_rstd(first, mom1, rstd1, nmr1, rstd1_ready, nmr1_ready)
            dve.wait_ge(nmr1_ready, 1)
            for t in (2, 3):
                nc.vector.tensor_scalar(xn[:, t], x_in[0][:, t], rstd1[:, t:t + 1], nmr1[:, t:t + 1],
                                        ALU.mult, ALU.add).then_inc(xn_ready, 1)
            dve.wait_ge(wv_landed, WV_LOADS)
            nc.vector.tensor_copy(Wvh[:, :, 0:D], wvT_sb[:]).then_inc(weight_hi, 1)
            dve.wait_ge(weight_hi, 1)
            nc.vector.tensor_tensor(Wvl[:, :, 0:D], wvT_sb[:], f32(Wvh[:, :, 0:D]), ALU.subtract)
            dve.wait_ge(m0h_ready, 1)
            nc.vector.tensor_tensor(M0l[:], ps[:, 2:4, 0:D], f32(M0h[:]), ALU.subtract)
            nc.vector.tensor_copy(Wvh[:, :, D], ps[:, 2:4, D]).then_inc(weight_hi, 1)
            dve.wait_ge(weight_hi, 2)
            nc.vector.tensor_tensor(Wvl[:, :, D], ps[:, 2:4, D], f32(Wvh[:, :, D]), ALU.subtract).then_inc(m0_ready, 1)
            hT_lo(first, 0)
            hT_lo(first, 1)
            dve.wait_ge(bias_psum, 1)
            nc.vector.tensor_copy(sbias[:], ps[:, 4, 0:KD])
            nc.vector.tensor_copy(bqbk[:], ps[:, 4, KD:KD + 1]).then_inc(bias_ready, 1)
            dve.wait_ge(bias_ready, 1)
            steps(dve, step, finish)

        @block.tensor
        def _(pe):
            def product(out_ap, pairs, done, pair_ready=None):
                last = 3 * len(pairs) - 1
                i = 0
                for q, ((ah, al), (bh, bl)) in enumerate(pairs):
                    if pair_ready is not None and pair_ready[q] is not None:
                        pe.wait_ge(*pair_ready[q])
                    for a, b_ in ((ah, bh), (ah, bl), (al, bh)):
                        mm = nc.tensor.matmul(out_ap, a, b_, start=(i == 0), stop=(i == last))
                        i += 1
                mm.then_inc(done, 1)

            def transposed_rows(src, done):
                for k in range(KD):
                    for t in range(T):
                        mm = nc.tensor.transpose(ps[:, BANK_TR + k, t * P:(t + 1) * P],
                                                 src[:, t, k * P:(k + 1) * P], ident[:])
                    mm.then_inc(done, 1)

            def TX(m):
                pe.wait_ge(xn_ready, m.count(4, 4))
                transposed_rows(xn, hT_psum)

            def project(wh, wl, inh, inl, k, done, halves_ready=None):
                product(ps[:, BANK_PROJ + k],
                        [((wh[:, q, k * P:(k + 1) * P], wl[:, q, k * P:(k + 1) * P]), (inh[:, q], inl[:, q]))
                         for q in range(KD)], done, halves_ready)

            def scores(ah, al, bh, bl, t, bank, done, halves_ready=None):
                product(ps[:, bank],
                        [((ah[:, q, t * P:(t + 1) * P], al[:, q, t * P:(t + 1) * P]), (bh[:, q], bl[:, q]))
                         for q in range(KD)], done, halves_ready)

            def both_halves(ready, n):
                return (ready, n.count(2, 1)), (ready, n.count(2, 2))

            def S(n, t):
                if t % 2 == 0:
                    pe.wait_ge(e_ready, n.count(2, t // 2 + 1))
                scores(sTh, sTl, hTh, hTl, t, BANK_S[t], s_psum, both_halves(sTl_ready, n) if t == 0 else None)

            def project_s2T(b, h2h=h2Th, h2l=h2Tl):
                project(M1h, M1l, h2h, h2l, 0, s2T_psum, both_halves(h2Tl_ready, b))
                project(M1h, M1l, h2h, h2l, 1, s2T_psum)

            def S2(n, b, t):
                pe.wait_ge(exp_ready, n.count(4, t + 1))
                scores(h2Th, h2Tl, s2Th, s2Tl, t, BANK_S[t], s2_psum, both_halves(s2Tl_ready, b) if t == 0 else None)

            def S2_last(b, t):
                if t == 3:
                    pe.wait_ge(soft_ready, b.count(1, 0))
                scores(hTh, hTl, s2Th, s2Tl, t, BANK_S2_LAST[t], s2_psum,
                       both_halves(s2Tl_ready, b) if t == 0 else None)

            def PV(n, t, last_pair_ready=None):
                if t == 0:
                    pe.wait_ge(v_ones, 1)
                    pe.wait_ge(vl_ready, n.count(2, 2))
                if t >= 2:
                    pe.wait_ge(x1_ready, n.count(4, t - 1))
                rows = slice(t * P, (t + 1) * P)
                product(ps[:, BANK_PROJ + t % 2, 0:VC],
                        [((Ph[:, j, rows], Pl[:, j, rows]), (vh[:, j], vl[:, j])) for j in range(T)], pv_psum,
                        [(pl_ready, n.count(4, j + 1)) for j in range(T)] if t == 0 else
                        [None] * (T - 1) + [last_pair_ready] if last_pair_ready else None)

            def V2(tiles=range(T), h2h=h2Th, h2l=h2Tl, first_bank=BANK_V2):
                for t in tiles:
                    rows = slice(t * P, (t + 1) * P)
                    product(v2_rows(t, first_bank),
                            [((h2h[:, q, rows], h2l[:, q, rows]), (W1h[:, q], W1l[:, q])) for q in range(KD)], v2_psum)

            def w_transposed(b):
                pe.wait_ge(wlog_ready, b.count(1, 1))
                nc.tensor.transpose(small[0:T, 0:P], w_log[:], ident[:]).then_inc(wlogT_psum, 1)

            def maxima(b):
                nc.tensor.transpose(small[:, MAX_COL:MAX_COL + T], neg_max4[:], ident[0:T, 0:T]).then_inc(max_psum, 1)

            def exp_sum(b):
                pe.wait_ge(wexp_ready, b.count(1, 1))
                nc.tensor.matmul(small[:, SUM_COL:SUM_COL + 1], ones[:], w_sum[:], start=True, stop=True
                                 ).then_inc(sum_psum, 1)

            def TX2(b):
                pe.wait_ge(xn2_ready, b.count(4, 4))
                transposed_rows(xn2, h2T_psum)

            def step(n, b, m):
                if b is not None:
                    pe.wait_ge(x1_ready, b.count(4, 3))
                project(M0h, M0l, hTh, hTl, 0, sT_psum, both_halves(hTl_ready, n))
                if b is not None:
                    pe.wait_ge(x1_ready, b.count(4, 4))
                project(M0h, M0l, hTh, hTl, 1, sT_psum)
                if b is None:
                    pe.wait_ge(bias_ready, 1)
                else:
                    pe.wait_ge(m1_ready, 1)
                    pe.wait_ge(scaled_mask_ready, 1)
                    pe.wait_ge(sv_ready, b.count(4, 4))
                for t in range(T):
                    product(ps[:, BANK_V + t, 0:VC],
                            [((hTh[:, q, t * P:(t + 1) * P], hTl[:, q, t * P:(t + 1) * P]), (Wvh[:, q], Wvl[:, q]))
                             for q in range(KD)], v_psum)
                if b is not None:
                    TX2(b)
                S(n, 0)
                S(n, 1)
                if b is not None:
                    project_s2T(b)
                S(n, 2)
                S(n, 3)
                if b is None:
                    layer1_weights()
                    TX(m)
                    for t in range(T):
                        PV(n, t)
                elif m is not None:
                    for t in range(T):
                        S2(n, b, t)
                    PV(n, 0)
                    PV(n, 1)
                    w_transposed(b)
                    TX(m)
                    PV(n, 2, last_pair_ready=(negmax4_ready, b.count(1, 1)))
                    maxima(b)
                    PV(n, 3)
                    V2(tiles=(0, 1))
                    exp_sum(b)
                    V2(tiles=(2, 3))
                else:
                    S2(n, b, 0)
                    S2(n, b, 1)
                    for t in range(T):
                        PV(n, t)
                    S2(n, b, 2)
                    S2(n, b, 3)
                    pe.wait_ge(w_ready, b.count(4, 2))
                    V2(tiles=(0, 1, 2))

            def finish(b, last):
                TX2(last)
                V2(tiles=(3,))
                w_transposed(b)
                project_s2T(last, hTh, hTl)
                pe.wait_ge(negmax4_ready, b.count(1, 1))
                maxima(b)
                V2(tiles=(0, 1), h2h=hTh, h2l=hTl, first_bank=BANK_V2_LAST)
                S2_last(last, 0)
                exp_sum(b)
                for t in range(1, T):
                    S2_last(last, t)
                V2(tiles=(2, 3), h2h=hTh, h2l=hTl, first_bank=BANK_V2_LAST)
                w_transposed(last)
                pe.wait_ge(negmax4_ready, last.count(1, 1))
                maxima(last)
                exp_sum(last)

            def layer1_weights():
                pe.wait_ge(late_landed, LATE_LOADS)
                pe.wait_ge(exp_ready, 2)
                for k in range(KD):
                    for q in range(KD):
                        nc.tensor.matmul(ps[:, 5, k * D:(k + 1) * D], wqkT_sb[:, KD + q, k * P:(k + 1) * P],
                                         wqkT_sb[:, q], start=(q == 0), stop=(q == KD - 1))
                nc.tensor.transpose(ps[:, 4, 0:B * T], mask_rows[:], ident[0:B * T, 0:B * T]).then_inc(m1_psum, 1)

            pe.wait_ge(const_ready, 4)
            pe.wait_ge(w0_landed, W0_LOADS)
            for k in range(KD):
                for q in range(KD):
                    mm = nc.tensor.matmul(ps[:, 2 + k, 0:D + 1], wk_sb[:, q, k * P:(k + 1) * P], wq_bq[:, q],
                                          start=(q == 0), stop=(q == KD - 1))
            mm.then_inc(m0_psum, 1)
            TX(batch(0))
            for k in range(KD):
                for q in range(KD):
                    nc.tensor.matmul(ps[:, 4, k:k + 1], wq_bq[:, q, k * P:(k + 1) * P], bk_col[:, q:q + 1],
                                     start=(q == 0), stop=(q == KD - 1))
            pe.wait_ge(bqbk_ready, 1)
            for q in range(KD):
                mm = nc.tensor.matmul(ps[:, 4, KD:KD + 1], ones[:], bqbk_col[:, q:q + 1],
                                      start=(q == 0), stop=(q == KD - 1))
            mm.then_inc(bias_psum, 1)
            pe.wait_ge(m0_ready, 1)
            steps(pe, step, finish)


def kernel(x, adj, nodemask, L0_gnn_Wq_w, L0_gnn_Wq_b, L0_gnn_Wk_w, L0_gnn_Wk_b, L0_gnn_Wv_w, L0_gnn_Wv_b,
           L1_gnn_Wqk, L1_gnn_Wv):
    import numpy as np
    import concourse.bacc as bacc
    from concourse.bass_utils import run_bass_kernel_spmd

    arrays = {
        "x": x, "adj": adj, "adjT": np.transpose(adj, (0, 2, 1)), "nodemask": nodemask,
        "wq": L0_gnn_Wq_w, "bq": L0_gnn_Wq_b, "wk": L0_gnn_Wk_w, "bk": L0_gnn_Wk_b,
        "wvT": np.transpose(L0_gnn_Wv_w), "bv": L0_gnn_Wv_b,
        "wqkT": np.transpose(L1_gnn_Wqk), "wv1": L1_gnn_Wv,
    }
    arrays = {name: np.ascontiguousarray(a) for name, a in arrays.items()}
    nc = bacc.Bacc("TRN2", target_bir_lowering=False, num_devices=1)
    ins = [nc.dram_tensor(name, a.shape, F32, kind="ExternalInput").ap() for name, a in arrays.items()]
    out = nc.dram_tensor("out", x.shape, F32, kind="ExternalOutput").ap()
    graph_layers_kernel(nc, *ins, out)
    result = run_bass_kernel_spmd(nc, [arrays], core_ids=[0])
    return result.results[0]["out"]
```
